# Optimizing a Trainium2 kernel written in Bass

```python
import numpy as np
import jax
import jax.numpy as jnp

def _softmax(x, axis=-1):
    return jax.nn.softmax(x, axis=axis)

def _gelu(x):
    return jax.nn.gelu(x, approximate=True)

def _silu(x):
    return jax.nn.silu(x)

def _sigmoid(x):
    return jax.nn.sigmoid(x)

def _layernorm(x, axis=-1, eps=1e-05):
    m = jnp.mean(x, axis=axis, keepdims=True)
    v = jnp.var(x, axis=axis, keepdims=True)
    return (x - m) / jnp.sqrt(v + eps)

def _scatter_add(tgt, idx, src, axis=0):
    return tgt.at[idx].add(src)

def _segment_sum(src, seg, n):
    return jax.ops.segment_sum(src, seg, n)
kernel_name = 'mk_cond_resid_d4_seqx_r8_f3dd64'

def setup_inputs(seed: int=0):
    np.random.seed(seed)
    _w = jnp.asarray

    def _rec_inputs():
        import jax
        import jax.numpy as jnp
        _rk = jax.random.key(seed)
        x = 0.5 + 0.2887 * jax.random.normal(jax.random.fold_in(_rk, 1), (32, 32, 128), jnp.float32)
        _lenS = 32 - jax.random.randint(jax.random.fold_in(_rk, 7), (32,), 0, max(1, 32 // 4) + 1, jnp.int32)
        _lenS2 = 32 - jax.random.randint(jax.random.fold_in(_rk, 8), (32,), 0, max(1, 32 // 4) + 1, jnp.int32)
        condB_zX = jax.random.uniform(jax.random.fold_in(_rk, 11), (32,), jnp.float32, 0.0, 0.983423)
        condB_zY = jax.random.uniform(jax.random.fold_in(_rk, 12), (32,), jnp.float32, 0.0, 0.979075)
        condB_zR = jax.random.uniform(jax.random.fold_in(_rk, 13), (32,), jnp.float32, 0.0, 0.9968)
        itok_B_0_7 = jax.random.randint(jax.random.fold_in(_rk, 14), (32,), 0, 8, jnp.int32)
        itok_B_0_2 = jax.random.randint(jax.random.fold_in(_rk, 15), (32,), 0, 3, jnp.int32)
        return (x, condB_zX, condB_zY, condB_zR, itok_B_0_7, itok_B_0_2)
    x, condB_zX, condB_zY, condB_zR, itok_B_0_7, itok_B_0_2 = _rec_inputs()

    def _L0_cond_setup():
        import jax, jax.numpy as jnp
        import numpy as np
        key = jax.random.key(seed)
        k1, k2, k3, k4 = jax.random.split(key, 4)
        B, H, W = (64, 128, 128)
        return {'y': jax.random.uniform(k1, (B, H, W), dtype=jnp.float32), 'zX': jax.random.uniform(k2, (B, 1), dtype=jnp.float32), 'zY': jax.random.uniform(k3, (B, 1), dtype=jnp.float32), 'zR': jax.random.uniform(k4, (B, 1), dtype=jnp.float32), 'dx': 1, 'dy': 1}
    _L0_cond_all = _L0_cond_setup()
    _L0_cond_in = {k: v for k, v in _L0_cond_all.items() if k in ()}
    del _L0_cond_all

    def _L1_cond_setup():
        import jax, jax.numpy as jnp
        import numpy as np
        S, O, H = (8, 128, 128)
        B, N = (32, 64)
        key = jax.random.key(seed)
        k1, k2, k3, k4 = jax.random.split(key, 4)
        x = jax.random.normal(k1, (B, N, H), dtype=jnp.float32)
        subject_id = jax.random.randint(k2, (B,), 0, S)
        wbound = jnp.sqrt(2.0 / 6.0) * jnp.sqrt(3.0 / H)
        weight = jax.random.uniform(k3, (S, O, H), minval=-wbound, maxval=wbound, dtype=jnp.float32)
        bbound = 1.0 / jnp.sqrt(H)
        bias = jax.random.uniform(k4, (S, O), minval=-bbound, maxval=bbound, dtype=jnp.float32)
        return {'x': x, 'subject_id': subject_id, 'weight': weight, 'bias': bias}
    _L1_cond_all = _L1_cond_setup()
    _L1_cond_in = {k: v for k, v in _L1_cond_all.items() if k in ('weight', 'bias')}
    del _L1_cond_all

    def _L2_cond_setup():
        import jax, jax.numpy as jnp
        import numpy as np
        B, S, D, F = (32, 64, 128, 512)
        R_COMMON, R_DOMAIN, E = (16, 16, 8)
        ALPHA = 2.0

        def _expert_lora(x, expert_ids, Wa, Wb):
            Ab = Wa[expert_ids]
            Bb = Wb[expert_ids]
            low = jnp.einsum('bsd,brd->bsr', x, Ab)
            return ALPHA * jnp.einsum('bsr,bor->bso', low, Bb)
        key = jax.random.key(seed)
        ks = jax.random.split(key, 12)
        sd = lambda k, shape: jax.random.normal(k, shape, dtype=jnp.float32) * (1.0 / np.sqrt(shape[-1]))
        return {'hidden_states': jax.random.normal(ks[0], (B, S, D), dtype=jnp.float32), 'expert_ids': jax.random.randint(ks[1], (B,), 0, E, dtype=jnp.int32), 'wi': sd(ks[2], (F, D)), 'wo': sd(ks[3], (D, F)), 'common_wi_a': sd(ks[4], (R_COMMON, D)), 'common_wi_b': sd(ks[5], (F, R_COMMON)), 'common_wo_a': sd(ks[6], (R_COMMON, F)), 'common_wo_b': sd(ks[7], (D, R_COMMON)), 'experts_wi_a': sd(ks[8], (E, R_DOMAIN, D)), 'experts_wi_b': sd(ks[9], (F, R_DOMAIN)) * jnp.ones((E, 1, 1)) * 0.0 + sd(ks[9], (E, F, R_DOMAIN)), 'experts_wo_a': sd(ks[10], (E, R_DOMAIN, F)), 'experts_wo_b': sd(ks[11], (E, D, R_DOMAIN))}
    _L2_cond_all = _L2_cond_setup()
    _L2_cond_in = {k: v for k, v in _L2_cond_all.items() if k in ('wi', 'wo', 'common_wi_a', 'common_wi_b', 'common_wo_a', 'common_wo_b', 'experts_wi_a', 'experts_wi_b', 'experts_wo_a', 'experts_wo_b')}
    del _L2_cond_all

    def _L3_cond_setup():
        import jax, jax.numpy as jnp
        import numpy as np
        NEG_INF = -1e+30
        key = jax.random.key(seed)
        k1, k2, k3, k4, k5 = jax.random.split(key, 5)
        B, S, D, A = (16, 128, 128, 32)
        hidden = jax.random.normal(k1, (B, S, D), dtype=jnp.float32)
        W1 = jax.random.normal(k2, (D, A), dtype=jnp.float32) / np.sqrt(D)
        b1 = jax.random.normal(k3, (A,), dtype=jnp.float32) * 0.01
        v = jax.random.normal(k4, (A,), dtype=jnp.float32) / np.sqrt(A)
        prompt_type_ids = jax.random.randint(k5, (B,), 0, 3, dtype=jnp.int32)
        return {'hidden': hidden, 'W1': W1, 'b1': b1, 'v': v, 'prompt_type_ids': prompt_type_ids}
    _L3_cond_all = _L3_cond_setup()
    _L3_cond_in = {k: v for k, v in _L3_cond_all.items() if k in ('W1', 'b1', 'v')}
    del _L3_cond_all
    return {'x': x, 'condB_zX': condB_zX, 'condB_zY': condB_zY, 'condB_zR': condB_zR, 'itok_B_0_7': itok_B_0_7, 'itok_B_0_2': itok_B_0_2, 'L1_cond_weight': _L1_cond_in['weight'], 'L1_cond_bias': _L1_cond_in['bias'], 'L2_cond_wi': _L2_cond_in['wi'], 'L2_cond_wo': _L2_cond_in['wo'], 'L2_cond_common_wi_a': _L2_cond_in['common_wi_a'], 'L2_cond_common_wi_b': _L2_cond_in['common_wi_b'], 'L2_cond_common_wo_a': _L2_cond_in['common_wo_a'], 'L2_cond_common_wo_b': _L2_cond_in['common_wo_b'], 'L2_cond_experts_wi_a': _L2_cond_in['experts_wi_a'], 'L2_cond_experts_wi_b': _L2_cond_in['experts_wi_b'], 'L2_cond_experts_wo_a': _L2_cond_in['experts_wo_a'], 'L2_cond_experts_wo_b': _L2_cond_in['experts_wo_b'], 'L3_cond_W1': _L3_cond_in['W1'], 'L3_cond_b1': _L3_cond_in['b1'], 'L3_cond_v': _L3_cond_in['v']}

def reference(x, condB_zX, condB_zY, condB_zR, itok_B_0_7, itok_B_0_2, L1_cond_weight, L1_cond_bias, L2_cond_wi, L2_cond_wo, L2_cond_common_wi_a, L2_cond_common_wi_b, L2_cond_common_wo_a, L2_cond_common_wo_b, L2_cond_experts_wi_a, L2_cond_experts_wi_b, L2_cond_experts_wo_a, L2_cond_experts_wo_b, L3_cond_W1, L3_cond_b1, L3_cond_v):
    import jax
    import jax.numpy as jnp

    def _L0_cond_ref(y, zX, zY, zR, dx, dy):
        import jax, jax.numpy as jnp
        import numpy as np
        yp_x = jnp.pad(y, ((0, 0), (0, 0), (1, 1)), mode='reflect')
        lap_x = (yp_x[:, :, :-2] - 2.0 * y + yp_x[:, :, 2:]) / (dx * dx)
        yp_y = jnp.pad(y, ((0, 0), (1, 1), (0, 0)), mode='reflect')
        lap_y = (yp_y[:, :-2, :] - 2.0 * y + yp_y[:, 2:, :]) / (dy * dy)
        du_dt = zX[:, :, None] * lap_x + zY[:, :, None] * lap_y + zR[:, :, None] * y * (1.0 - y)
        return du_dt

    def _L1_cond_ref(x, subject_id, weight, bias):
        import jax, jax.numpy as jnp
        import numpy as np
        S, O, H = (8, 128, 128)
        B, N = (32, 64)
        W = weight[subject_id]
        b = bias[subject_id]
        y = jnp.einsum('bnh,boh->bno', x, W) + b[:, None, :]
        return y

    def _L2_cond_ref(hidden_states, expert_ids, wi, wo, common_wi_a, common_wi_b, common_wo_a, common_wo_b, experts_wi_a, experts_wi_b, experts_wo_a, experts_wo_b):
        import jax, jax.numpy as jnp
        import numpy as np
        B, S, D, F = (32, 64, 128, 512)
        R_COMMON, R_DOMAIN, E = (16, 16, 8)
        ALPHA = 2.0

        def _expert_lora(x, expert_ids, Wa, Wb):
            Ab = Wa[expert_ids]
            Bb = Wb[expert_ids]
            low = jnp.einsum('bsd,brd->bsr', x, Ab)
            return ALPHA * jnp.einsum('bsr,bor->bso', low, Bb)
        x = hidden_states
        hidden_i = jnp.einsum('bsd,fd->bsf', x, wi)
        hidden_i += ALPHA * jnp.einsum('bsr,fr->bsf', jnp.einsum('bsd,rd->bsr', x, common_wi_a), common_wi_b)
        hidden_i += _expert_lora(x, expert_ids, experts_wi_a, experts_wi_b)
        hidden_i = jax.nn.relu(hidden_i)
        hidden_o = jnp.einsum('bsf,df->bsd', hidden_i, wo)
        hidden_o += ALPHA * jnp.einsum('bsr,dr->bsd', jnp.einsum('bsf,rf->bsr', hidden_i, common_wo_a), common_wo_b)
        hidden_o += _expert_lora(hidden_i, expert_ids, experts_wo_a, experts_wo_b)
        return hidden_o

    def _L3_cond_ref(hidden, W1, b1, v, prompt_type_ids):
        import jax, jax.numpy as jnp
        import numpy as np
        NEG_INF = -1e+30
        B, S, D = hidden.shape
        attn_in = jnp.tanh(jnp.einsum('bsd,da->bsa', hidden, W1) + b1)
        scores = jnp.einsum('bsa,a->bs', attn_in, v)
        idx = jnp.arange(S)
        j = idx[:, None]
        l = idx[None, :]
        prefix_m = l <= j
        postfix_m = l >= j
        cloze_m = l != j
        pt = prompt_type_ids[:, None, None]
        mask = jnp.where(pt == 0, prefix_m[None], jnp.where(pt == 1, postfix_m[None], cloze_m[None]))
        masked_scores = jnp.where(mask, scores[:, None, :], NEG_INF)
        p = jax.nn.softmax(masked_scores, axis=-1)
        cnt = jnp.sum(mask, axis=-1).astype(hidden.dtype)
        pooled = jnp.einsum('bjl,bld->bjd', p, hidden) / cnt[..., None]
        return pooled
    x = x + _L0_cond_ref(x, condB_zX[:, None], condB_zY[:, None], condB_zR[:, None], 1, 1)
    x = x + _L1_cond_ref(x, itok_B_0_7, L1_cond_weight, L1_cond_bias)
    x = x + _L2_cond_ref(x, itok_B_0_7, L2_cond_wi, L2_cond_wo, L2_cond_common_wi_a, L2_cond_common_wi_b, L2_cond_common_wo_a, L2_cond_common_wo_b, L2_cond_experts_wi_a, L2_cond_experts_wi_b, L2_cond_experts_wo_a, L2_cond_experts_wo_b)
    x = x + _L3_cond_ref(x, L3_cond_W1, L3_cond_b1, L3_cond_v, itok_B_0_2)
    return x

_drawn_inputs = setup_inputs


def setup_inputs(seed=0):
    import zlib

    import numpy as np

    out = dict(_drawn_inputs(seed))
    spreads = {}
    factors = {'L3_cond_b1': 200.0, 'L3_cond_v': 2.7}
    for name, (base, spread) in spreads.items():
        noise = np.random.default_rng([zlib.crc32(name.encode()), seed]).standard_normal(out[name].shape)
        drawn = base * np.exp(spread * noise) if base else spread * noise
        out[name] = jnp.asarray(drawn.astype(out[name].dtype))
    for name, factor in factors.items():
        out[name] = (out[name] * factor).astype(out[name].dtype)
    return out
```

```python
import concourse.bass as bass
from concourse import mybir
from contextlib import ExitStack

F32 = mybir.dt.float32
I32 = mybir.dt.int32
ALU = mybir.AluOpType
ACT = mybir.ActivationFunctionType
AX = mybir.AxisListType

B, S, D = 32, 32, 128
E, R, F, A = 8, 16, 512, 32
P = 128
Q = P // S
G = B // Q
NC = 2
GC = G // NC
T = GC * P
K = F // P
WORD = 8
ALPHA = 2.0
NEG = -1e30

COL_Z = {"zX": 0, "zY": G, "zR": 2 * G}
COL_I = 3 * G
COL_STENCIL = COL_I + P
COL_E = COL_STENCIL + P
COL_ROW = COL_E + 1
COL_POW = COL_ROW + 1
N_FIRST = COL_POW + B
COL_A1, COL_WI, COL_B1 = 0, P, P + F
N_IN = P + 2 * F
COL_WO, COL_A2, COL_B2 = 0, K * D, 2 * K * D
N_OUT = 2 * K * D + D
COL_CA, COL_CB, COL_COA, COL_COB = 0, D, D + F, D + 2 * F
N_COMMON = 2 * D + 2 * F
COL_W1, COL_V, COL_B1L3, COL_PEN, COL_CNT = 0, A, A + P, A + P + 1, A + P + 1 + 3 * S
N_POOL = COL_CNT + 3


def program(nc, first, ids, x_tok, w_subject, b_subject, common, w_in, w_out, pool_in, out):
    with ExitStack() as ctx:
        def sb(name, shape, dt=F32):
            return ctx.enter_context(nc.sbuf_tensor(name, shape, dt))

        def sem(name):
            return ctx.enter_context(nc.semaphore(name))

        first_sb = sb("first_sb", [P, N_FIRST])
        ids_sb = sb("ids_sb", [P, B + G], I32)
        x_sb = sb("x_sb", [P, NC, GC, D])
        wsub = sb("wsub", [P, E * D])
        bsub = sb("bsub", [E, D])
        com = sb("com", [R, N_COMMON])
        win = sb("win", [P, N_IN])
        wout = sb("wout", [P, N_OUT])
        pin = sb("pin", [P, N_POOL])
        ident = first_sb[:, COL_I:COL_I + P]
        stencil = first_sb[:, COL_STENCIL:COL_STENCIL + P]

        coef = sb("coef", [P, 3, G])
        m_lin = sb("m_lin", [P, G, P])
        m_dx = sb("m_dx", [P, G, P])
        m_dr = sb("m_dr", [P, G, P])
        nbr = sb("nbr", [P, NC, GC, D])
        xsq = sb("xsq", [P, NC, GC, D])
        prod = sb("prod", [1, B])
        words = sb("words", [1, B // WORD], I32)
        hot = sb("hot", [E, B])
        expert = sb("expert", [P, B])
        bias = sb("bias", [P, B])
        x1q = sb("x1q", [P, Q, G, P])
        x1b = sb("x1b", [P, NC, T])
        y = sb("y", [P, NC, GC, D])
        x2 = sb("x2", [P, NC, T])
        wi = sb("wi", [P, F])
        wo = sb("wo", [P, K, D])
        low = sb("low", [P, NC, T])
        h = sb("h", [P, NC, K, T])
        low2 = sb("low2", [P, NC, T])
        x3 = sb("x3", [P, NC, T])
        is_type = sb("is_type", [P, 2, G])
        pen_part = sb("pen_part", [P, 2, G, S])
        pen_sum = sb("pen_sum", [P, G, S])
        pen = sb("pen", [P, G, S])
        cnt_part = sb("cnt_part", [P, 2, G])
        cnt_sum = sb("cnt_sum", [P, G])
        cnt = sb("cnt", [P, G])
        attn = sb("attn", [P, NC, GC * S])
        sm = sb("sm", [P, NC, GC, S])
        smax = sb("smax", [P, NC, GC])
        sd = sb("sd", [P, NC, GC, S])
        e = sb("e", [P, NC, GC, S])
        esum = sb("esum", [P, NC, GC])
        den = sb("den", [P, NC, GC])
        rden = sb("rden", [P, NC, GC])
        et = sb("et", [P, G, Q, S])
        x3n = sb("x3n", [P, NC, GC, D])
        res = sb("res", [P, NC, GC, D])

        bank = [ctx.enter_context(nc.psum_tensor(f"bank{i}", [P, T], F32)) for i in range(8)]
        PS_X1 = [bank[0], bank[1]]
        PS_Y = [bank[2], bank[3]]
        PS_HID = [bank[4], bank[5], bank[2]]
        PS_LOW, PS_OUT = bank[6], bank[7]
        PS_SC = bank[3]

        names = ("d_first d_ids d_x0 d_x1 d_wsub d_bsub d_common d_win d_wout d_pool d_out "
                 "coef_t coef_ready icoef_ready lin_ready dx_ready dr_ready nbr_ready xsq_ready "
                 "prod_ready words_ready masks_ready bias_done bias_ready wi_done wo_done wi_ready wo_ready "
                 "zeroed et_zeroed x1_done x1q_ready x1b_ready y_done y_ready yt_done x2_ready "
                 "low_done low_ready hid_done h_ready low2_done low2_ready out_done x3_ready "
                 "type_ready pen_part_ready pen_sum_ready pen_ready cnt_ready attn_done attn_ready score_done sm_ready "
                 "smax_ready sd_ready e_ready esum_ready den_ready rden_ready et_ready x3n_done x3n_ready "
                 "pooled_done res_ready").split()
        s = {n: sem(n) for n in names}
        block = ctx.enter_context(nc.Block())

        def bcast(ap, axis, shape):
            return ap.unsqueeze(axis).to_broadcast(shape)

        def per_batch(ap):
            return bcast(ap, 2, [P, GC * Q, S])

        def batches(ap):
            return ap.rearrange("p (b s) -> p b s", s=S)

        @block.sync
        def _(sp):
            sp.dma_start(ids_sb[:], ids).then_inc(s["d_ids"], 16)
            sp.dma_start(first_sb[:], first).then_inc(s["d_first"], 16)
            for c in range(NC):
                sp.dma_start(x_sb[:, c], x_tok[c].rearrange("p (g d) -> p g d", g=GC)).then_inc(s[f"d_x{c}"], 16)
            sp.dma_start(wsub[:], w_subject).then_inc(s["d_wsub"], 16)
            sp.dma_start(wout[:], w_out).then_inc(s["d_wout"], 16)
            for c in range(NC):
                sp.wait_ge(s["res_ready"], GC * (c + 1))
                sp.dma_start(out[c].rearrange("p (g d) -> p g d", g=GC), res[:, c]).then_inc(s["d_out"], 16)
            sp.wait_ge(s["d_out"], 16 * NC)

        @block.gpsimd
        def _(pool):
            for c in range(NC):
                pool.memset(x1q[:, :, GC * c:GC * (c + 1), :], 0.0).then_inc(s["zeroed"], 1)
                if c == 0:
                    pool.wait_ge(s["d_first"], 16)
                    z = first_sb[:, COL_Z["zX"]:COL_Z["zX"] + G]
                    for cc in range(NC):
                        gs = slice(GC * cc, GC * (cc + 1))
                        pool.tensor_tensor(m_dx[:, gs], bcast(ident, 1, [P, GC, P]), bcast(z[:, gs], 2, [P, GC, P]),
                                           ALU.mult).then_inc(s["dx_ready"], 1)
            pool.memset(et[:], 0.0).then_inc(s["et_zeroed"], 1)
            pool.wait_ge(s["type_ready"], 2)
            pool.wait_ge(s["d_pool"], 16)
            for k in range(2):
                one = is_type[:, k]
                pk = pin[:, COL_PEN + (k + 1) * S:COL_PEN + (k + 2) * S]
                pool.tensor_tensor(pen_part[:, k], bcast(pk, 1, [P, G, S]), bcast(one, 2, [P, G, S]),
                                   ALU.mult).then_inc(s["pen_part_ready"], 1)
            pool.wait_ge(s["pen_part_ready"], 2)
            pool.tensor_tensor(pen_sum[:], pen_part[:, 0], pen_part[:, 1], ALU.add).then_inc(s["pen_sum_ready"], 1)
            pool.wait_ge(s["pen_sum_ready"], 1)
            pool.tensor_tensor(pen[:], pen_sum[:], bcast(pin[:, COL_PEN:COL_PEN + S], 1, [P, G, S]),
                               ALU.add).then_inc(s["pen_ready"], 1)

        @block.scalar
        def _(act):
            act.dma_start(com[:], common).then_inc(s["d_common"], 16)
            act.dma_start(bsub[:], b_subject).then_inc(s["d_bsub"], 16)
            act.dma_start(win[:], w_in).then_inc(s["d_win"], 16)
            act.dma_start(pin[:], pool_in).then_inc(s["d_pool"], 16)
            for c in range(NC):
                act.wait_ge(s[f"d_x{c}"], 16)
                act.activation(xsq[:, c], x_sb[:, c], ACT.Square).then_inc(s["xsq_ready"], 1)
            for c in range(NC):
                act.wait_ge(s["x1_done"], c + 1)
                act.wait_ge(s["zeroed"], c + 1)
                src = PS_X1[c][:].rearrange("p (g q s) -> p q g s", g=GC, q=Q)
                for q in range(Q):
                    act.copy(x1q[:, q, GC * c:GC * (c + 1), S * q:S * (q + 1)], src[:, q]).then_inc(s["x1q_ready"], 1)
            for c in range(NC):
                act.wait_ge(s["y_done"], c + 1)
                act.copy(y[:, c], PS_Y[c][:].rearrange("p (g d) -> p g d", g=GC)).then_inc(s["y_ready"], 1)
            for c in range(NC):
                for k in range(K):
                    act.wait_ge(s["hid_done"], K * c + k + 1)
                    act.activation(h[:, c, k], PS_HID[(K * c + k) % 3][:], ACT.Relu).then_inc(s["h_ready"], 1)
                act.wait_ge(s["attn_done"], c + 1)
                act.wait_ge(s["d_pool"], 16)
                act.activation(attn[:, c], PS_X1[0][:, 0:GC * S], ACT.Tanh,
                               bias=pin[:, COL_B1L3:COL_B1L3 + 1]).then_inc(s["attn_ready"], 1)
                act.wait_ge(s["x3n_done"], c + 1)
                act.copy(x3n[:, c], PS_X1[1][:].rearrange("p (g d) -> p g d", g=GC)).then_inc(s["x3n_ready"], 1)
                act.wait_ge(s["sd_ready"], c + 1)
                act.activation(e[:, c], sd[:, c], ACT.Exp).then_inc(s["e_ready"], 1)

        @block.vector
        def _(dve):
            dve.wait_ge(s["d_ids"], 16)
            dve.wait_ge(s["d_first"], 16)
            dve.tensor_tensor(prod[:], ids_sb[0:1, 0:B], first_sb[0:1, COL_POW:COL_POW + B],
                              ALU.mult).then_inc(s["prod_ready"], 1)
            zX, zY, zR = (first_sb[:, COL_Z[n]:COL_Z[n] + G] for n in ("zX", "zY", "zR"))
            dve.scalar_tensor_tensor(out=coef[:, 0], in0=zX, scalar=-2.0, in1=zR, op0=ALU.mult,
                                     op1=ALU.add).then_inc(s["coef_t"], 1)
            dve.tensor_scalar(coef[:, 1], zR, -1.0, None, ALU.mult).then_inc(s["coef_t"], 1)
            dve.wait_ge(s["prod_ready"], 1)
            with nc.allow_low_precision(reason="whole numbers below 2 ** 24 are exact in the float32 sum"):
                dve.tensor_reduce(words[:], prod[:].rearrange("p (w k) -> p w k", k=WORD), AX.X,
                                  ALU.add).then_inc(s["words_ready"], 1)
            dve.wait_ge(s["coef_t"], 2)
            dve.tensor_scalar(coef[:, 2], coef[:, 0], 1.0, None, ALU.add).then_inc(s["coef_ready"], 1)
            dve.wait_ge(s["coef_ready"], 1)
            for c in range(NC):
                for g in range(GC * c, GC * (c + 1)):
                    dve.tensor_scalar(m_lin[:, g], ident, coef[:, 2, g:g + 1], None, ALU.mult).then_inc(s["icoef_ready"], 1)
                    dve.tensor_scalar(m_dr[:, g], ident, coef[:, 1, g:g + 1], None, ALU.mult).then_inc(s["dr_ready"], 1)
                for g in range(GC * c, GC * (c + 1)):
                    dve.wait_ge(s["icoef_ready"], g + 1)
                    dve.scalar_tensor_tensor(out=m_lin[:, g], in0=stencil, scalar=zY[:, g:g + 1], in1=m_lin[:, g],
                                             op0=ALU.mult, op1=ALU.add).then_inc(s["lin_ready"], 1)
                dve.wait_ge(s[f"d_x{c}"], 16)
                dve.tensor_tensor(nbr[:, c, :, 1:D - 1], x_sb[:, c, :, 0:D - 2], x_sb[:, c, :, 2:D],
                                  ALU.add).then_inc(s["nbr_ready"], 1)
                dve.tensor_scalar(nbr[:, c, :, 0:D:D - 1], x_sb[:, c, :, 1:D - 1:D - 3], 2.0, None,
                                  ALU.mult).then_inc(s["nbr_ready"], 1)
                if c == 0:
                    dve.tensor_scalar(hot[:], ids_sb[0:E, 0:B], first_sb[0:E, COL_ROW:COL_ROW + 1], None,
                                      ALU.is_equal).then_inc(s["masks_ready"], 1)
                    dve.tensor_scalar(expert[:], ids_sb[:, 0:B], first_sb[:, COL_E:COL_E + 1], ALPHA,
                                      ALU.is_equal, ALU.mult).then_inc(s["masks_ready"], 1)
                    for k in range(2):
                        dve.tensor_scalar(is_type[:, k], ids_sb[:, B:B + G], float(k), None,
                                          ALU.is_equal).then_inc(s["type_ready"], 1)
            dve.wait_ge(s["bias_done"], 1)
            dve.tensor_copy(bias[:], PS_OUT[:, 0:B]).then_inc(s["bias_ready"], 1)
            dve.wait_ge(s["wi_done"], 1)
            dve.wait_ge(s["d_win"], 16)
            dve.scalar_tensor_tensor(out=wi[:], in0=PS_HID[0][:], scalar=ALPHA, in1=win[:, COL_WI:COL_WI + F],
                                     op0=ALU.mult, op1=ALU.add).then_inc(s["wi_ready"], 1)
            dve.wait_ge(s["wo_done"], 1)
            dve.wait_ge(s["d_wout"], 16)
            dve.scalar_tensor_tensor(out=wo[:], in0=PS_HID[1][:].rearrange("p (k d) -> p k d", k=K), scalar=ALPHA,
                                     in1=wout[:, COL_WO:COL_WO + K * D].rearrange("p (k d) -> p k d", k=K),
                                     op0=ALU.mult, op1=ALU.add).then_inc(s["wo_ready"], 1)
            dve.wait_ge(s["bias_ready"], 1)
            for c in range(NC):
                dve.wait_ge(s["x1q_ready"], Q * (c + 1))
                bs = slice(GC * Q * c, GC * Q * (c + 1))
                dve.tensor_tensor(batches(x1b[:, c]), batches(PS_X1[c][:]), per_batch(bias[:, bs]),
                                  ALU.add).then_inc(s["x1b_ready"], 1)
            cnt_cols = pin[:, COL_CNT:COL_CNT + 3]
            dve.wait_ge(s["d_pool"], 16)
            dve.wait_ge(s["type_ready"], 2)
            for k in range(2):
                dve.tensor_scalar(cnt_part[:, k], is_type[:, k], cnt_cols[:, k + 1:k + 2], None,
                                  ALU.mult).then_inc(s["cnt_ready"], 1)
            dve.wait_ge(s["cnt_ready"], 2)
            dve.tensor_tensor(cnt_sum[:], cnt_part[:, 0], cnt_part[:, 1], ALU.add).then_inc(s["cnt_ready"], 1)
            dve.wait_ge(s["cnt_ready"], 3)
            dve.tensor_scalar(cnt[:], cnt_sum[:], cnt_cols[:, 0:1], None, ALU.add).then_inc(s["cnt_ready"], 1)
            for c in range(NC):
                dve.wait_ge(s["yt_done"], c + 1)
                dve.wait_ge(s["x1b_ready"], c + 1)
                dve.tensor_tensor(x2[:, c], PS_X1[c][:], x1b[:, c], ALU.add).then_inc(s["x2_ready"], 1)
            for c in range(NC):
                bs = slice(GC * Q * c, GC * Q * (c + 1))
                dve.wait_ge(s["low_done"], c + 1)
                dve.wait_ge(s["masks_ready"], 2)
                dve.tensor_tensor(batches(low[:, c]), batches(PS_LOW[:]), per_batch(expert[:, bs]),
                                  ALU.mult).then_inc(s["low_ready"], 1)
                dve.wait_ge(s["low2_done"], c + 1)
                dve.tensor_tensor(batches(low2[:, c]), batches(PS_LOW[:]), per_batch(expert[:, bs]),
                                  ALU.mult).then_inc(s["low2_ready"], 1)
                dve.wait_ge(s["out_done"], c + 1)
                dve.tensor_tensor(x3[:, c], PS_OUT[:], x2[:, c], ALU.add).then_inc(s["x3_ready"], 1)
                dve.wait_ge(s["score_done"], c + 1)
                dve.wait_ge(s["pen_ready"], 1)
                dve.tensor_tensor(sm[:, c], PS_SC[:, 0:GC * S].rearrange("p (g l) -> p g l", g=GC),
                                  pen[:, GC * c:GC * (c + 1)], ALU.add).then_inc(s["sm_ready"], 1)
                dve.wait_ge(s["sm_ready"], c + 1)
                dve.tensor_reduce(smax[:, c], sm[:, c], AX.X, ALU.max).then_inc(s["smax_ready"], 1)
                dve.wait_ge(s["smax_ready"], c + 1)
                dve.tensor_tensor(sd[:, c], sm[:, c], bcast(smax[:, c], 2, [P, GC, S]),
                                  ALU.subtract).then_inc(s["sd_ready"], 1)
                dve.wait_ge(s["e_ready"], c + 1)
                dve.wait_ge(s["et_zeroed"], 1)
                for q in range(Q):
                    qs = slice(S * q, S * (q + 1))
                    dve.transpose(et[qs, GC * c:GC * (c + 1), q, :], e[qs, c]).then_inc(s["et_ready"], 1)
                dve.tensor_reduce(esum[:, c], e[:, c], AX.X, ALU.add).then_inc(s["esum_ready"], 1)
                dve.wait_ge(s["esum_ready"], c + 1)
                dve.wait_ge(s["cnt_ready"], 4)
                dve.tensor_tensor(den[:, c], esum[:, c], cnt[:, GC * c:GC * (c + 1)], ALU.mult).then_inc(s["den_ready"], 1)
                dve.wait_ge(s["den_ready"], c + 1)
                dve.reciprocal(rden[:, c], den[:, c]).then_inc(s["rden_ready"], 1)
                dve.wait_ge(s["rden_ready"], c + 1)
                dve.wait_ge(s["pooled_done"], c + 1)
                dve.wait_ge(s["x3n_ready"], c + 1)
                for g in range(GC):
                    dve.scalar_tensor_tensor(out=res[:, c, g], in0=PS_X1[0][:, P * g:P * (g + 1)],
                                             scalar=rden[:, c, g:g + 1], in1=x3n[:, c, g], op0=ALU.mult,
                                             op1=ALU.add).then_inc(s["res_ready"], 1)

        @block.tensor
        def _(pe):
            pe.wait_ge(s["d_common"], 16)
            pe.matmul(PS_HID[0][:], com[:, COL_CA:COL_CA + D], com[:, COL_CB:COL_CB + F],
                      start=True, stop=True).then_inc(s["wi_done"], 1)
            for k in range(K):
                last = pe.matmul(PS_HID[1][:, D * k:D * (k + 1)], com[:, COL_COA + P * k:COL_COA + P * (k + 1)],
                                 com[:, COL_COB:COL_COB + D], start=True, stop=True)
            last.then_inc(s["wo_done"], 1)
            pe.wait_ge(s["d_bsub"], 16)
            pe.wait_ge(s["words_ready"], 1)
            _, loaded = nc.values_load_multi_w_load_instructions(
                words[0:1, :], engines=(pe.engine,), min_val=0, max_val=E ** WORD - 1)
            for c in range(NC):
                pe.wait_ge(s["lin_ready"], GC * (c + 1))
                pe.wait_ge(s["dr_ready"], GC * (c + 1))
                pe.wait_ge(s["dx_ready"], c + 1)
                pe.wait_ge(s[f"d_x{c}"], 16)
                pe.wait_ge(s["nbr_ready"], 2 * (c + 1))
                pe.wait_ge(s["xsq_ready"], c + 1)
                for g in range(GC):
                    o = PS_X1[c][:, P * g:P * (g + 1)]
                    pe.matmul(o, x_sb[:, c, g], m_lin[:, GC * c + g], start=True, stop=False)
                    pe.matmul(o, nbr[:, c, g], m_dx[:, GC * c + g], start=False, stop=False)
                    last = pe.matmul(o, xsq[:, c, g], m_dr[:, GC * c + g], start=False, stop=True)
                last.then_inc(s["x1_done"], 1)
                if c == 0:
                    pe.wait_ge(s["masks_ready"], 1)
                    pe.matmul(PS_OUT[:, 0:B], bsub[:], hot[:], start=True, stop=True).then_inc(s["bias_done"], 1)
            pe.wait_ge(s["d_wsub"], 16)
            for c in range(NC):
                pe.wait_ge(s["x1q_ready"], Q * (c + 1))
                for g in range(GC):
                    for q in range(Q):
                        b = Q * (GC * c + g) + q
                        number = (loaded[b // WORD] >> (3 * (b % WORD))) & (E - 1)
                        last = pe.matmul(PS_Y[c][:, D * g:D * (g + 1)], x1q[:, q, GC * c + g],
                                         wsub[:, bass.ds(number * D, D)], start=(q == 0), stop=(q == Q - 1))
                last.then_inc(s["y_done"], 1)
            for c in range(NC):
                pe.wait_ge(s["y_ready"], c + 1)
                pe.wait_ge(s["x1b_ready"], c + 1)
                for g in range(GC):
                    last = pe.transpose(PS_X1[c][:, P * g:P * (g + 1)], y[:, c, g], ident)
                last.then_inc(s["yt_done"], 1)
            pe.wait_ge(s["d_win"], 16)
            pe.wait_ge(s["d_wout"], 16)
            pe.wait_ge(s["wi_ready"], 1)
            pe.wait_ge(s["wo_ready"], 1)
            pe.wait_ge(s["bias_ready"], 1)
            for c in range(NC):
                pe.wait_ge(s["x2_ready"], c + 1)
                if c:
                    pe.wait_ge(s["low2_ready"], c)
                pe.matmul(PS_LOW[:], win[:, COL_A1:COL_A1 + P], x2[:, c], start=True, stop=True).then_inc(s["low_done"], 1)

                def base(k):
                    n = K * c + k
                    if n >= 3:
                        pe.wait_ge(s["h_ready"], n - 2)
                    pe.matmul(PS_HID[n % 3][:], wi[:, P * k:P * (k + 1)], x2[:, c], start=True, stop=False)

                def lora(k):
                    pe.wait_ge(s["low_ready"], c + 1)
                    pe.matmul(PS_HID[(K * c + k) % 3][:], win[:, COL_B1 + P * k:COL_B1 + P * (k + 1)], low[:, c],
                              start=False, stop=True).then_inc(s["hid_done"], 1)

                def onward(k):
                    pe.wait_ge(s["h_ready"], K * c + k + 1)
                    if c and k == 0:
                        pe.wait_ge(s["x3_ready"], c)
                    pe.matmul(PS_OUT[:], wo[:, k], h[:, c, k], start=(k == 0), stop=False)
                    m = pe.matmul(PS_LOW[:], wout[:, COL_A2 + P * k:COL_A2 + P * (k + 1)], h[:, c, k],
                                  start=(k == 0), stop=(k == K - 1))
                    if k == K - 1:
                        m.then_inc(s["low2_done"], 1)

                base(0)
                base(1)
                lora(0)
                lora(1)
                base(2)
                lora(2)
                onward(0)
                base(3)
                lora(3)
                for k in range(1, K):
                    onward(k)
                pe.wait_ge(s["low2_ready"], c + 1)
                pe.matmul(PS_OUT[:], wout[:, COL_B2:COL_B2 + D], low2[:, c], start=False, stop=True).then_inc(s["out_done"], 1)

                pe.wait_ge(s["x3_ready"], c + 1)
                if c == 0:
                    pe.wait_ge(s["x2_ready"], NC)
                    pe.wait_ge(s["d_pool"], 16)
                else:
                    pe.wait_ge(s["res_ready"], GC * c)
                x3v = x3[:, c].rearrange("p (g q l) -> p q g l", g=GC, q=Q)
                for q in range(Q):
                    last = pe.matmul(PS_X1[0][S * q:S * (q + 1), 0:GC * S], pin[:, COL_W1:COL_W1 + A], x3v[:, q],
                                     start=True, stop=True)
                last.then_inc(s["attn_done"], 1)
                for g in range(GC):
                    last = pe.transpose(PS_X1[1][:, P * g:P * (g + 1)], x3[:, c, P * g:P * (g + 1)], ident)
                last.then_inc(s["x3n_done"], 1)
                pe.wait_ge(s["attn_ready"], c + 1)
                pe.matmul(PS_SC[:, 0:GC * S], pin[:, COL_V:COL_V + P], attn[:, c],
                          start=True, stop=True).then_inc(s["score_done"], 1)
                pe.wait_ge(s["et_ready"], Q * (c + 1))
                pe.wait_ge(s["x3n_ready"], c + 1)
                for g in range(GC):
                    last = pe.matmul(PS_X1[0][:, P * g:P * (g + 1)], et[:, GC * c + g].rearrange("p q l -> p (q l)"),
                                     x3n[:, c, g], start=True, stop=True)
                last.then_inc(s["pooled_done"], 1)


def kernel(x, condB_zX, condB_zY, condB_zR, itok_B_0_7, itok_B_0_2, L1_cond_weight, L1_cond_bias, L2_cond_wi,
           L2_cond_wo, L2_cond_common_wi_a, L2_cond_common_wi_b, L2_cond_common_wo_a, L2_cond_common_wo_b,
           L2_cond_experts_wi_a, L2_cond_experts_wi_b, L2_cond_experts_wo_a, L2_cond_experts_wo_b, L3_cond_W1,
           L3_cond_b1, L3_cond_v):
    import numpy as np
    import concourse.bacc as bacc
    from concourse.bass_utils import run_bass_kernel_spmd

    f32 = np.float32

    def side(*parts):
        return np.ascontiguousarray(np.concatenate([np.asarray(p) for p in parts], axis=1))

    def per_token(z):
        return np.repeat(np.asarray(z).reshape(G, Q).T, S, axis=0)

    row = np.arange(P)
    stencil = np.zeros((P, P), f32)
    for t in range(P):
        s = t % S
        stencil[t, t] = -2.0
        stencil[t - 1 if s else t + 1, t] += 1.0
        stencil[t + 1 if s < S - 1 else t - 1, t] += 1.0
    j, l = np.meshgrid(row % S, np.arange(S), indexing="ij")
    prefix, postfix, cloze = (np.where(m, 0.0, NEG) for m in (l <= j, l >= j, l != j))
    n_prefix, n_cloze = (row % S + 1)[:, None], np.full((P, 1), S - 1)
    powers = np.tile(float(E) ** (np.arange(B) % WORD), (P, 1))

    arrays = {
        "first": side(per_token(condB_zX), per_token(condB_zY), per_token(condB_zR), np.eye(P, dtype=f32), stencil,
                      (row // R)[:, None].astype(f32), row[:, None].astype(f32), powers.astype(f32)),
        "ids": side(np.tile(np.asarray(itok_B_0_7), (P, 1)), per_token(itok_B_0_2)),
        "x_tok": np.asarray(x).reshape(NC, GC, Q, S, D).transpose(0, 2, 3, 1, 4).reshape(NC, P, GC * D),
        "w_subject": np.asarray(L1_cond_weight).transpose(2, 0, 1).reshape(D, E * D),
        "b_subject": np.asarray(L1_cond_bias),
        "common": side(L2_cond_common_wi_a, np.asarray(L2_cond_common_wi_b).T, L2_cond_common_wo_a,
                       np.asarray(L2_cond_common_wo_b).T),
        "w_in": side(np.asarray(L2_cond_experts_wi_a).reshape(E * R, D).T, np.asarray(L2_cond_wi).T,
                     np.asarray(L2_cond_experts_wi_b).transpose(0, 2, 1).reshape(E * R, F)),
        "w_out": side(np.asarray(L2_cond_wo).T.reshape(K, P, D).transpose(1, 0, 2).reshape(P, K * D),
                      np.asarray(L2_cond_experts_wo_a).transpose(2, 0, 1).reshape(K, P, E * R)
                      .transpose(1, 0, 2).reshape(P, K * E * R),
                      np.asarray(L2_cond_experts_wo_b).transpose(0, 2, 1).reshape(E * R, D)),
        "pool_in": side(L3_cond_W1, _score_weights(np.asarray(L3_cond_v), np),
                        np.tile(np.asarray(L3_cond_b1), Q)[:, None],
                        cloze.astype(f32), (prefix - cloze).astype(f32), (postfix - cloze).astype(f32),
                        n_cloze.astype(f32), (n_prefix - n_cloze).astype(f32),
                        (S + 1 - n_prefix - n_cloze).astype(f32)),
    }
    nc = bacc.Bacc("TRN2", target_bir_lowering=False, num_devices=1)
    args = []
    for name, a in arrays.items():
        a = arrays[name] = np.ascontiguousarray(a)
        args.append(nc.dram_tensor(name, a.shape, mybir.dt.from_np(a.dtype), kind="ExternalInput").ap())
    out = nc.dram_tensor("out", (NC, P, GC * D), F32, kind="ExternalOutput").ap()
    program(nc, *args, out)
    got = run_bass_kernel_spmd(nc, [arrays], core_ids=[0]).results[0]["out"]
    return got.reshape(NC, Q, S, GC, D).transpose(0, 3, 1, 2, 4).reshape(B, S, D)


def _score_weights(v, np):
    w = np.zeros((P, P), v.dtype)
    for q in range(Q):
        w[A * q:A * (q + 1), S * q:S * (q + 1)] = v[:, None]
    return w
```

```python
import concourse.bass as bass
from concourse import mybir
from contextlib import ExitStack

F32 = mybir.dt.float32
F32R = mybir.dt.float32r
I32 = mybir.dt.int32
ALU = mybir.AluOpType
ACT = mybir.ActivationFunctionType
AX = mybir.AxisListType

B, S, D = 32, 32, 128
E, R, F, A = 8, 16, 512, 32
P = 128
Q = P // S
G = B // Q
NC = 2
GC = G // NC
T = GC * P
NU = 4
GU = G // NU
BU = B // NU
TU = T * NC // NU
K = F // P
ROWS = 32
HELP = 3
WORD = 8
ALPHA = 2.0
NEG = -1e30


def columns(**widths):
    at, out = 0, {}
    for name, n in widths.items():
        out[name] = slice(at, at + n)
        at += n
    return out, at


PARTS = [(0, BU), (BU, BU), (2 * BU, 2 * BU)]
WARM = 7
IDS, N_IDS = columns(subject=B, mask=G, power=B)
FIRST, N_FIRST = columns(zX=B, zY=B, zR=B, row=1, expert=1, second=D)
SUBJECT, N_SUBJECT = columns(w=E * D, ident=P)
COMMON, N_COMMON = columns(wi_a=D, wi_b=F, wo_a=F, wo_b=D, bias=D)
W_IN, N_IN = columns(a=E * R, base=F)
W_OUT, N_OUT = columns(base=K * D, a=K * E * R, b=D)
POOL, N_POOL = columns(w1=A, v=P, b1=1, penalty=3 * S, count=3)


SEMAPHORES = [
    "d_x0", "d_ids", "d_common", "d_x1", "d_wout", "d_pool", "res_ready", "d_out", "grow_ready", "rest_ready",
    "x1_ready", "x1b_ready", "et_zeroed", "d_first", "centre_ready", "d_win", "a1h_ready", "a1l_ready",
    "bias_ready", "d_bin", "b1h_ready", "b1l_ready", "a2h_ready", "a2l_ready", "type_ready", "pen_part_ready",
    "pen_sum_ready", "pen_ready", "wb_ready", "y_done", "y_ready", "x2_ready", "x2h_ready", "low_ready",
    "lowh_ready", "hid_done", "hh_ready", "attn_done", "attn_ready", "x3n_done", "x3n_ready", "sd_ready",
    "e_ready", "d_wsub", "warm_ready", "words_ready", "wi_ready", "wih_ready", "wo_ready", "woh_ready",
    "near_ready", "along_ready", "second_done", "across_ready", "react_ready", "sums_ready", "yt_done",
    "x2l_ready", "low_done", "lowl_ready", "hl_ready", "mid_done", "mid_ready", "out_done", "x3_ready",
    "score_done", "smax_ready", "et_ready", "esum_ready", "den_ready", "rden_ready", "pooled_done",
    "zeros_ready", "centre_t_ready", "prod_ready", "hot_ready", "wi_done", "bias_done", "expert_ready", "scaled_ready", "res_first", "wb_helped",
    "wil_ready", "wo_done", "wol_ready", "cnt_part_ready", "cnt_sum_ready", "cnt_ready",
]


def program(nc, ids, first, x_t, w_subject, common, w_in, b_in, w_out, pool_in, out):
    with ExitStack() as ctx:
        def sb(name, shape, dt=F32):
            return ctx.enter_context(nc.sbuf_tensor(name, shape, dt))

        def sem(name):
            return ctx.enter_context(nc.semaphore(name))

        ids_sb = sb("ids_sb", [P, N_IDS], I32)
        first_sb = sb("first_sb", [P, N_FIRST])
        x = sb("x", [P, B, S])
        wsub = sb("wsub", [P, N_SUBJECT])
        com = sb("com", [ROWS, N_COMMON])
        win = sb("win", [P, N_IN])
        bin_ = sb("bin_", [P, F])
        wout = sb("wout", [P, N_OUT])
        pin = sb("pin", [P, N_POOL])
        ident = wsub[:, SUBJECT["ident"]]
        zX, zY, zR = (first_sb[:, FIRST[n]] for n in ("zX", "zY", "zR"))

        warm = sb("warm", [P, 1])
        warmed = sb("warmed", [P, 1])
        zeros = sb("zeros", [P, T])
        centre_t = sb("centre_t", [P, B])
        centre = sb("centre", [P, B])
        near = sb("near", [P, B, S])
        along = sb("along", [P, B, S])
        grow = sb("grow", [P, B, S])
        rest = sb("rest", [P, B, S])
        react = sb("react", [P, B, S])
        across = sb("across", [P, B, S])
        sums = sb("sums", [P, B, S])
        x1 = sb("x1", [P, B, S])
        prod = sb("prod", [1, B])
        words = sb("words", [1, B // WORD], I32)
        hot = sb("hot", [ROWS, B])
        expert = sb("expert", [P, B])
        bias = sb("bias", [P, B])
        wb = sb("wb", [P, B, D])
        x1b = sb("x1b", [P, B, S])
        y = sb("y", [P, G, D])
        x2 = sb("x2", [P, NC * T])
        x2h = sb("x2h", [P, NC * T], F32R)
        x2l = sb("x2l", [P, NC * T], F32R)
        a1h, a1l = sb("a1h", [P, E * R], F32R), sb("a1l", [P, E * R], F32R)
        b1h, b1l = sb("b1h", [P, F], F32R), sb("b1l", [P, F], F32R)
        wi, wih, wil = sb("wi", [P, F]), sb("wih", [P, F], F32R), sb("wil", [P, F], F32R)
        wo, woh, wol = sb("wo", [P, K * D]), sb("woh", [P, K * D], F32R), sb("wol", [P, K * D], F32R)
        a2h, a2l = sb("a2h", [P, K * E * R], F32R), sb("a2l", [P, K * E * R], F32R)
        low, lowh, lowl = sb("low", [P, NC * T]), sb("lowh", [P, NC * T], F32R), sb("lowl", [P, NC * T], F32R)
        hh, hl = sb("hh", [P, NC, K, T], F32R), sb("hl", [P, NC, K, T], F32R)
        mid = sb("mid", [P, NC * T])
        x3 = sb("x3", [P, NC * T])
        is_type = sb("is_type", [P, 2, G])
        pen_part = sb("pen_part", [P, 2, G, S])
        pen_sum = sb("pen_sum", [P, G, S])
        pen = sb("pen", [P, G, S])
        cnt_part = sb("cnt_part", [P, 2, G])
        cnt_sum = sb("cnt_sum", [P, G])
        cnt = sb("cnt", [P, G])
        attn = sb("attn", [P, G, S])
        smax = sb("smax", [P, G])
        sd = sb("sd", [P, G, S])
        e = sb("e", [P, G, S])
        esum = sb("esum", [P, G])
        den = sb("den", [P, G])
        rden = sb("rden", [P, G])
        et = sb("et", [P, G, Q, S])
        x3n = sb("x3n", [P, G, D])
        scaled = sb("scaled", [P, GC, D])
        res = sb("res", [P, G, D])

        bank = [ctx.enter_context(nc.psum_tensor(f"bank{i}", [P, T], F32)) for i in range(8)]
        PS_DIFF = [bank[0], bank[1], bank[5]]
        PS_YT = [bank[0], bank[1], bank[0], bank[1]]
        PS_Y = [bank[2], bank[3], bank[3], bank[3]]
        PS_HID = [bank[i] for i in (4, 2, 5, 1, 4, 2, 5, 4)]
        PS_LOW = [bank[6], bank[3]]
        PS_WARM, PS_WI, PS_WO, PS_BIAS = bank[5], bank[4], bank[7], bank[6]
        STEPS = [dict(g0=0, n=GC, out=bank[7], mid=bank[6], attn=bank[0], turn=bank[1], score=bank[3], pool=bank[2]),
                 dict(g0=GC, n=GC // 2, out=bank[7], mid=bank[6], attn=bank[0], turn=bank[1], score=bank[5],
                      pool=bank[0]),
                 dict(g0=GC + GC // 2, n=GC // 2, out=bank[4], mid=bank[2], attn=bank[3], turn=bank[6], score=bank[7],
                      pool=bank[3])]

        s = {n: sem(n) for n in SEMAPHORES}
        block = ctx.enter_context(nc.Block())

        def bcast(ap, axis, shape):
            return ap.unsqueeze(axis).to_broadcast(shape)

        def over_batch(ap):
            return bcast(ap, 2, [P, ap.shape[1], S])

        def by_batch(ap):
            return ap.rearrange("p (b s) -> p b s", s=S)

        def f32(ap):
            return ap.bitcast(F32)

        def batches(u):
            return slice(BU * u, BU * (u + 1))

        def part(i):
            return slice(PARTS[i][0], PARTS[i][0] + PARTS[i][1])

        def tokens(u):
            return slice(TU * u, TU * (u + 1))

        def tiles(step):
            return slice(step["g0"], step["g0"] + step["n"])

        def step_tokens(step):
            return slice(P * step["g0"], P * (step["g0"] + step["n"]))

        def load_words(engine, w0, w1):
            engine.wait_ge(s["words_ready"], 1)
            return nc.values_load_multi_w_load_instructions(
                words[0:1, w0:w1], engines=(engine.engine,), min_val=0, max_val=(E ** WORD - 1) * D)[1]

        def place(engine, word, b):
            return engine.snap((word >> (3 * (b % WORD))) & ((E - 1) * D))

        @block.sync
        def _(sp):
            sp.dma_start(ids_sb[:], ids).then_inc(s["d_ids"], 16)
            sp.dma_start(x[:, 0:B // 2], by_batch(x_t[:, 0:T])).then_inc(s["d_x0"], 16)
            sp.dma_start(com[:], common).then_inc(s["d_common"], 16)
            sp.dma_start(win[:], w_in).then_inc(s["d_win"], 16)
            sp.dma_start(bin_[:], b_in).then_inc(s["d_bin"], 16)
            sp.dma_start(x[:, B // 2:B], by_batch(x_t[:, T:2 * T])).then_inc(s["d_x1"], 16)
            sp.dma_start(wout[:], w_out).then_inc(s["d_wout"], 16)
            sp.dma_start(pin[:], pool_in).then_inc(s["d_pool"], 16)
            for n, (ready, count) in ((1, ("res_ready", 2)), (0, ("res_first", 2)), (2, ("res_ready", 4))):
                sp.wait_ge(s[ready], count)
                sp.dma_start(out[:, tiles(STEPS[n])], res[:, tiles(STEPS[n])]).then_inc(s["d_out"], 16)
            sp.wait_ge(s["d_out"], 16 * len(STEPS))

        @block.gpsimd
        def _(pool):
            def rate(i):
                bs = part(i)
                pool.tensor_tensor(grow[:, bs], x[:, bs], over_batch(zR[:, bs]), ALU.mult).then_inc(s["grow_ready"], 1)
                pool.wait_ge(s["grow_ready"], i + 1)
                pool.tensor_tensor(rest[:, bs], over_batch(centre[:, bs]), grow[:, bs], ALU.subtract)\
                    .then_inc(s["rest_ready"], 1)

            def add_bias(i):
                bs = part(i)
                pool.wait_ge(s["x1_ready"], i + 1)
                pool.tensor_tensor(x1b[:, bs], x1[:, bs], over_batch(bias[:, bs]), ALU.add).then_inc(s["x1b_ready"], 1)

            pool.memset(et[:], 0.0).then_inc(s["et_zeroed"], 1)
            (word,) = load_words(pool, 1, 2)
            helped = [(b, place(pool, word, b)) for b in range(2 * BU - HELP, 2 * BU)]
            pool.wait_ge(s["d_first"], 16)
            pool.wait_ge(s["centre_ready"], 1)
            pool.wait_ge(s["d_x0"], 16)
            rate(0)
            rate(1)
            pool.wait_ge(s["d_wsub"], 16)
            for b, at in helped:
                last = pool.tensor_copy(wb[:, b], wsub[:, bass.ds(at, D)])
            last.then_inc(s["wb_helped"], 1)
            pool.wait_ge(s["bias_ready"], 1)
            add_bias(0)
            add_bias(1)
            pool.wait_ge(s["d_win"], 16)
            pool.wait_ge(s["a1h_ready"], 1)
            pool.tensor_tensor(a1l[:], win[:, W_IN["a"]], f32(a1h[:]), ALU.subtract).then_inc(s["a1l_ready"], 1)
            pool.wait_ge(s["wih_ready"], 1)
            pool.tensor_tensor(wil[:], wi[:], f32(wih[:]), ALU.subtract).then_inc(s["wil_ready"], 1)
            pool.wait_ge(s["d_x1"], 16)
            rate(2)
            pool.wait_ge(s["d_bin"], 16)
            pool.wait_ge(s["b1h_ready"], 1)
            pool.tensor_tensor(b1l[:], bin_[:], f32(b1h[:]), ALU.subtract).then_inc(s["b1l_ready"], 1)
            pool.wait_ge(s["d_wout"], 16)
            pool.wait_ge(s["a2h_ready"], 1)
            pool.tensor_tensor(a2l[:], wout[:, W_OUT["a"]], f32(a2h[:]), ALU.subtract).then_inc(s["a2l_ready"], 1)
            pool.wait_ge(s["woh_ready"], 1)
            pool.tensor_tensor(wol[:], wo[:], f32(woh[:]), ALU.subtract).then_inc(s["wol_ready"], 1)
            add_bias(2)
            pool.wait_ge(s["type_ready"], 2)
            pool.wait_ge(s["d_pool"], 16)
            penalty = pin[:, POOL["penalty"]].rearrange("p (k l) -> p k l", k=3)
            for k in range(2):
                pool.tensor_tensor(pen_part[:, k], bcast(penalty[:, k + 1], 1, [P, G, S]),
                                   bcast(is_type[:, k], 2, [P, G, S]), ALU.mult).then_inc(s["pen_part_ready"], 1)
            pool.wait_ge(s["pen_part_ready"], 2)
            pool.tensor_tensor(pen_sum[:], pen_part[:, 0], pen_part[:, 1], ALU.add).then_inc(s["pen_sum_ready"], 1)
            pool.wait_ge(s["pen_sum_ready"], 1)
            pool.tensor_tensor(pen[:], pen_sum[:], bcast(penalty[:, 0], 1, [P, G, S]), ALU.add)\
                .then_inc(s["pen_ready"], 1)
            pool.wait_ge(s["x3n_ready"], 1)
            for h in range(2):
                gs = slice(GC // 2 * h, GC // 2 * (h + 1))
                pool.wait_ge(s["scaled_ready"], gs.stop)
                pool.tensor_tensor(res[:, gs], scaled[:, gs], x3n[:, gs], ALU.add).then_inc(s["res_first"], 1)

        @block.scalar
        def _(act):
            def gather(b0, b1):
                for b in range(b0, b1):
                    at = place(act, loaded[b // WORD], b)
                    act.copy(wb[:, b], wsub[:, bass.ds(at, D)]).then_inc(s["wb_ready"], 1)

            def copy_y(u):
                act.wait_ge(s["y_done"], u + 1)
                act.copy(y[:, GU * u:GU * (u + 1)], PS_Y[u][:, 0:TU].rearrange("p (g d) -> p g d", g=GU))\
                    .then_inc(s["y_ready"], 1)

            def split_x2(u):
                act.wait_ge(s["x2_ready"], u + 1)
                act.copy(x2h[:, tokens(u)], x2[:, tokens(u)]).then_inc(s["x2h_ready"], 1)

            def split_low(c):
                act.wait_ge(s["low_ready"], c + 1)
                act.copy(lowh[:, T * c:T * (c + 1)], low[:, T * c:T * (c + 1)]).then_inc(s["lowh_ready"], 1)

            def relu(c, k):
                act.wait_ge(s["hid_done"], K * c + k + 1)
                act.activation(hh[:, c, k], PS_HID[K * c + k][:], ACT.Relu).then_inc(s["hh_ready"], 1)

            def tanh(n):
                step = STEPS[n]
                act.wait_ge(s["attn_done"], n + 1)
                act.activation(attn[:, tiles(step)].rearrange("p g l -> p (g l)"), step["attn"][:, 0:S * step["n"]],
                               ACT.Tanh, bias=pin[:, POOL["b1"]]).then_inc(s["attn_ready"], 1)

            def copy_x3n(n):
                step = STEPS[n]
                act.wait_ge(s["x3n_done"], n + 1)
                act.copy(x3n[:, tiles(step)], step["turn"][:, 0:P * step["n"]].rearrange("p (g d) -> p g d", d=D))\
                    .then_inc(s["x3n_ready"], 1)

            def exp(n):
                act.wait_ge(s["sd_ready"], n + 1)
                act.activation(e[:, tiles(STEPS[n])], sd[:, tiles(STEPS[n])], ACT.Exp).then_inc(s["e_ready"], 1)

            def scale_pooled(n, i0, i1):
                step = STEPS[n]
                act.wait_ge(s["rden_ready"], n + 1)
                act.wait_ge(s["pooled_done"], step["g0"] + step["n"])
                for i in range(i0, i1):
                    g = step["g0"] + i
                    act.activation(scaled[:, g], step["pool"][:, P * i:P * (i + 1)], ACT.Copy, scale=rden[:, g:g + 1])\
                        .then_inc(s["scaled_ready"], 1)

            act.dma_start(first_sb[:], first).then_inc(s["d_first"], 16)
            act.dma_start(wsub[:], w_subject).then_inc(s["d_wsub"], 16)
            act.wait_ge(s["warm_ready"], 1)
            act.activation(warmed[:], warm[:], ACT.Tanh)
            loaded = load_words(act, 0, NU)
            act.wait_ge(s["d_wsub"], 16)
            gather(0, 2 * BU - HELP)
            copy_y(0)
            act.wait_ge(s["d_win"], 16)
            act.copy(a1h[:], win[:, W_IN["a"]]).then_inc(s["a1h_ready"], 1)
            act.wait_ge(s["wi_ready"], 1)
            act.copy(wih[:], wi[:]).then_inc(s["wih_ready"], 1)
            copy_y(1)
            split_x2(0)
            act.wait_ge(s["d_bin"], 16)
            act.copy(b1h[:], bin_[:]).then_inc(s["b1h_ready"], 1)
            split_x2(1)
            gather(2 * BU, 2 * BU + 3)
            act.wait_ge(s["d_wout"], 16)
            act.copy(a2h[:], wout[:, W_OUT["a"]]).then_inc(s["a2h_ready"], 1)
            act.wait_ge(s["wo_ready"], 1)
            act.copy(woh[:], wo[:]).then_inc(s["woh_ready"], 1)
            split_low(0)
            gather(2 * BU + 3, 3 * BU)
            relu(0, 0)
            relu(0, 1)
            gather(3 * BU, 3 * BU + 4)
            relu(0, 2)
            copy_y(2)
            relu(0, 3)
            gather(3 * BU + 4, 4 * BU)
            split_x2(2)
            copy_y(3)
            split_x2(3)
            split_low(1)
            relu(1, 0)
            relu(1, 1)
            act.wait_ge(s["d_pool"], 16)
            tanh(0)
            relu(1, 2)
            copy_x3n(0)
            relu(1, 3)
            exp(0)
            tanh(1)
            copy_x3n(1)
            exp(1)
            tanh(2)
            copy_x3n(2)
            scale_pooled(0, 0, 3)
            exp(2)
            scale_pooled(0, 3, 4)

        @block.vector
        def _(dve):
            def along_sequence(i):
                neighbours(i)
                scale_neighbours(i)

            def neighbours(i):
                bs = part(i)
                dve.tensor_tensor(near[:, bs, 1:S - 1], x[:, bs, 0:S - 2], x[:, bs, 2:S], ALU.add)\
                    .then_inc(s["near_ready"], 1)
                dve.tensor_scalar(near[:, bs, 0:S:S - 1], x[:, bs, 1:S - 1:S - 3], 2.0, None, ALU.mult)\
                    .then_inc(s["near_ready"], 1)

            def scale_neighbours(i):
                bs = part(i)
                dve.wait_ge(s["near_ready"], 2 * (i + 1))
                dve.tensor_tensor(along[:, bs], near[:, bs], over_batch(zY[:, bs]), ALU.mult)\
                    .then_inc(s["along_ready"], 1)

            def scale_second(i):
                bs = part(i)
                dve.wait_ge(s["second_done"], i + 1)
                dve.tensor_tensor(across[:, bs], by_batch(PS_DIFF[i][:, 0:S * PARTS[i][1]]), over_batch(zX[:, bs]),
                                  ALU.mult).then_inc(s["across_ready"], 1)

            def diffuse(i):
                bs = part(i)
                dve.wait_ge(s["rest_ready"], i + 1)
                dve.tensor_tensor(react[:, bs], rest[:, bs], x[:, bs], ALU.mult).then_inc(s["react_ready"], 1)
                dve.wait_ge(s["along_ready"], i + 1)
                dve.wait_ge(s["across_ready"], i + 1)
                dve.tensor_tensor(sums[:, bs], along[:, bs], across[:, bs], ALU.add).then_inc(s["sums_ready"], 1)
                dve.wait_ge(s["sums_ready"], i + 1)
                dve.wait_ge(s["react_ready"], i + 1)
                dve.tensor_tensor(x1[:, bs], sums[:, bs], react[:, bs], ALU.add).then_inc(s["x1_ready"], 1)

            def add_x2(u):
                dve.wait_ge(s["yt_done"], u + 1)
                dve.wait_ge(s["x1b_ready"], min(u, 2) + 1)
                dve.tensor_tensor(by_batch(x2[:, tokens(u)]), by_batch(PS_YT[u][:, 0:TU]), x1b[:, batches(u)], ALU.add)\
                    .then_inc(s["x2_ready"], 1)

            def split_x2(u):
                ts = tokens(u)
                dve.wait_ge(s["x2h_ready"], u + 1)
                dve.tensor_tensor(x2l[:, ts], x2[:, ts], f32(x2h[:, ts]), ALU.subtract).then_inc(s["x2l_ready"], 1)

            def pick_low(c):
                bs = slice(B // NC * c, B // NC * (c + 1))
                dve.wait_ge(s["low_done"], c + 1)
                dve.tensor_tensor(by_batch(low[:, T * c:T * (c + 1)]), by_batch(PS_LOW[c][:]), over_batch(expert[:, bs]),
                                  ALU.mult).then_inc(s["low_ready"], 1)

            def split_low(c):
                ts = slice(T * c, T * (c + 1))
                dve.wait_ge(s["lowh_ready"], c + 1)
                dve.tensor_tensor(lowl[:, ts], low[:, ts], f32(lowh[:, ts]), ALU.subtract).then_inc(s["lowl_ready"], 1)

            def relu_rest(c, k):
                dve.wait_ge(s["hh_ready"], K * c + k + 1)
                dve.scalar_tensor_tensor(out=hl[:, c, k], in0=PS_HID[K * c + k][:], scalar=0.0,
                                         in1=f32(hh[:, c, k]), op0=ALU.max, op1=ALU.subtract).then_inc(s["hl_ready"], 1)

            def pick_mid(n):
                step = STEPS[n]
                bs = slice(Q * step["g0"], Q * (step["g0"] + step["n"]))
                dve.wait_ge(s["mid_done"], n + 1)
                dve.tensor_tensor(by_batch(mid[:, step_tokens(step)]), by_batch(step["mid"][:, 0:P * step["n"]]),
                                  over_batch(expert[:, bs]), ALU.mult).then_inc(s["mid_ready"], 1)

            def add_x3(n):
                step = STEPS[n]
                ts = step_tokens(step)
                dve.wait_ge(s["out_done"], n + 1)
                dve.tensor_tensor(x3[:, ts], step["out"][:, 0:P * step["n"]], x2[:, ts], ALU.add)\
                    .then_inc(s["x3_ready"], 1)

            def softmax(n):
                step = STEPS[n]
                gs, w = tiles(step), step["n"]
                masked = step["score"][:, 0:S * w].rearrange("p (g l) -> p g l", g=w)
                dve.wait_ge(s["score_done"], n + 1)
                dve.tensor_reduce(smax[:, gs], masked, AX.X, ALU.max).then_inc(s["smax_ready"], 1)
                dve.wait_ge(s["smax_ready"], n + 1)
                dve.tensor_tensor(sd[:, gs], masked, bcast(smax[:, gs], 2, [P, w, S]), ALU.subtract)\
                    .then_inc(s["sd_ready"], 1)

            def turn(n):
                gs = tiles(STEPS[n])
                dve.wait_ge(s["e_ready"], n + 1)
                for q in range(Q):
                    qs = slice(S * q, S * (q + 1))
                    last = dve.transpose(et[qs, gs, q, :], e[qs, gs])
                last.then_inc(s["et_ready"], 1)
                dve.tensor_reduce(esum[:, gs], e[:, gs], AX.X, ALU.add).then_inc(s["esum_ready"], 1)
                dve.wait_ge(s["esum_ready"], n + 1)
                dve.tensor_tensor(den[:, gs], esum[:, gs], cnt[:, gs], ALU.mult).then_inc(s["den_ready"], 1)
                dve.wait_ge(s["den_ready"], n + 1)
                dve.reciprocal(rden[:, gs], den[:, gs]).then_inc(s["rden_ready"], 1)

            def finish(n):
                step = STEPS[n]
                dve.wait_ge(s["rden_ready"], n + 1)
                dve.wait_ge(s["pooled_done"], step["g0"] + step["n"])
                dve.wait_ge(s["x3n_ready"], n + 1)
                for i in range(step["n"]):
                    g = step["g0"] + i
                    dve.scalar_tensor_tensor(out=res[:, g], in0=step["pool"][:, P * i:P * (i + 1)],
                                             scalar=rden[:, g:g + 1], in1=x3n[:, g], op0=ALU.mult,
                                             op1=ALU.add).then_inc(s["res_ready"], 1)

            dve.memset(zeros[:], 0.0).then_inc(s["zeros_ready"], 1)
            dve.memset(warm[:], 0.0).then_inc(s["warm_ready"], 1)
            dve.wait_ge(s["d_ids"], 16)
            dve.tensor_tensor(prod[:], ids_sb[0:1, IDS["subject"]], ids_sb[0:1, IDS["power"]], ALU.mult)\
                .then_inc(s["prod_ready"], 1)
            dve.wait_ge(s["prod_ready"], 1)
            with nc.allow_low_precision(reason="multiples of D below 2 ** 24 of it are exact in float32"):
                dve.tensor_reduce(words[:], prod[:].rearrange("p (w k) -> p w k", k=WORD), AX.X, ALU.add)\
                    .then_inc(s["words_ready"], 1)
            dve.wait_ge(s["d_first"], 16)
            dve.tensor_scalar(hot[:], ids_sb[0:ROWS, IDS["subject"]], first_sb[0:ROWS, FIRST["row"]], None, ALU.is_equal)\
                .then_inc(s["hot_ready"], 1)
            dve.scalar_tensor_tensor(out=centre_t[:], in0=zY, scalar=-2.0, in1=zR, op0=ALU.mult, op1=ALU.add)\
                .then_inc(s["centre_t_ready"], 1)
            dve.wait_ge(s["centre_t_ready"], 1)
            dve.tensor_scalar(centre[:], centre_t[:], 1.0, None, ALU.add).then_inc(s["centre_ready"], 1)
            dve.wait_ge(s["d_x0"], 16)
            along_sequence(0)
            neighbours(1)
            scale_second(0)
            diffuse(0)
            dve.wait_ge(s["bias_done"], 1)
            dve.tensor_copy(bias[:], PS_BIAS[:, 0:B]).then_inc(s["bias_ready"], 1)
            scale_neighbours(1)
            scale_second(1)
            diffuse(1)
            dve.wait_ge(s["wi_done"], 1)
            dve.wait_ge(s["d_win"], 16)
            dve.scalar_tensor_tensor(out=wi[:], in0=PS_WI[:], scalar=ALPHA, in1=win[:, W_IN["base"]],
                                     op0=ALU.mult, op1=ALU.add).then_inc(s["wi_ready"], 1)
            dve.wait_ge(s["d_x1"], 16)
            neighbours(2)
            dve.tensor_scalar(expert[:], ids_sb[:, IDS["subject"]], first_sb[:, FIRST["expert"]], ALPHA, ALU.is_equal,
                              ALU.mult).then_inc(s["expert_ready"], 1)
            add_x2(0)
            add_x2(1)
            split_x2(0)
            split_x2(1)
            dve.wait_ge(s["wo_done"], 1)
            dve.wait_ge(s["d_wout"], 16)
            dve.scalar_tensor_tensor(out=wo[:], in0=PS_WO[:], scalar=ALPHA, in1=wout[:, W_OUT["base"]],
                                     op0=ALU.mult, op1=ALU.add).then_inc(s["wo_ready"], 1)
            scale_second(2)
            dve.wait_ge(s["expert_ready"], 1)
            pick_low(0)
            scale_neighbours(2)
            split_low(0)
            diffuse(2)
            relu_rest(0, 0)
            for k in range(2):
                dve.tensor_scalar(is_type[:, k], ids_sb[:, IDS["mask"]], float(k), None, ALU.is_equal)\
                    .then_inc(s["type_ready"], 1)
            relu_rest(0, 1)
            relu_rest(0, 2)
            add_x2(2)
            relu_rest(0, 3)
            split_x2(2)
            add_x2(3)
            split_x2(3)
            count = pin[:, POOL["count"]]
            dve.wait_ge(s["d_pool"], 16)
            dve.wait_ge(s["type_ready"], 2)
            for k in range(2):
                dve.tensor_scalar(cnt_part[:, k], is_type[:, k], count[:, k + 1:k + 2], None, ALU.mult)\
                    .then_inc(s["cnt_part_ready"], 1)
            dve.wait_ge(s["cnt_part_ready"], 2)
            dve.tensor_tensor(cnt_sum[:], cnt_part[:, 0], cnt_part[:, 1], ALU.add).then_inc(s["cnt_sum_ready"], 1)
            dve.wait_ge(s["cnt_sum_ready"], 1)
            dve.tensor_scalar(cnt[:], cnt_sum[:], count[:, 0:1], None, ALU.add).then_inc(s["cnt_ready"], 1)
            pick_mid(0)
            pick_low(1)
            split_low(1)
            add_x3(0)
            relu_rest(1, 0)
            relu_rest(1, 1)
            relu_rest(1, 2)
            softmax(0)
            relu_rest(1, 3)
            dve.wait_ge(s["et_zeroed"], 1)
            dve.wait_ge(s["cnt_ready"], 1)
            turn(0)
            pick_mid(1)
            add_x3(1)
            pick_mid(2)
            softmax(1)
            add_x3(2)
            turn(1)
            softmax(2)
            finish(1)
            turn(2)
            finish(2)

        @block.tensor
        def _(pe):
            def product(o, wh, wl, vh, vl, start, stop, vl_ready):
                pe.matmul(o, wh, vh, start=start, stop=False)
                pe.matmul(o, wl, vh, start=False, stop=False)
                pe.wait_ge(*vl_ready)
                return pe.matmul(o, wh, vl, start=False, stop=stop)

            def keep_warm(n):
                for _ in range(n):
                    pe.matmul(PS_WARM[:, 0:P], zeros[:, 0:P], zeros[:, 0:P], start=True, stop=True)

            def second_difference(i, h):
                b0 = PARTS[i][0] + BU * h
                return pe.matmul(PS_DIFF[i][:, TU * h:TU * (h + 1)], first_sb[:, FIRST["second"]], x[:, b0:b0 + BU],
                                 start=True, stop=True)

            def common_out(k):
                wo_a = com[:, COMMON["wo_a"]]
                return pe.matmul(PS_WO[:, D * k:D * (k + 1)], wo_a[:, P * k:P * (k + 1)], com[:, COMMON["wo_b"]],
                                 start=True, stop=True)

            def subject(u):
                pe.wait_ge(s["wb_ready"], BU * (u + 1) - (HELP if u else 0))
                pe.wait_ge(s["x1_ready"], min(u, 2) + 1)
                if u >= 2:
                    pe.wait_ge(s["y_ready"], u)
                for g in range(GU):
                    for q in range(Q):
                        b = BU * u + Q * g + q
                        last = pe.matmul(PS_Y[u][S * q:S * (q + 1), D * g:D * (g + 1)], x1[:, b], wb[:, b],
                                         start=True, stop=True)
                last.then_inc(s["y_done"], 1)

            def turn_y(u):
                pe.wait_ge(s["y_ready"], u + 1)
                if PS_YT[u] is PS_HID[K - 1] and u >= 2:
                    pe.wait_ge(s["hl_ready"], K)
                for g in range(GU):
                    last = pe.transpose(PS_YT[u][:, P * g:P * (g + 1)], y[:, GU * u + g], ident)
                last.then_inc(s["yt_done"], 1)

            def chunk(c):
                return slice(T * c, T * (c + 1))

            def of_tokens(u0, u1):
                t0 = T * (TU * u0 // T)
                return slice(TU * u0 - t0, TU * u1 - t0), slice(TU * u0, TU * u1), (s["x2l_ready"], u1)

            def down(u0, u1):
                cols, ts, x2l_ready = of_tokens(u0, u1)
                pe.wait_ge(s["x2h_ready"], u1)
                if u0 >= NU // NC:
                    pe.wait_ge(s["y_ready"], NU)
                return product(PS_LOW[TU * u0 // T][:, cols], a1h[:], a1l[:], x2h[:, ts], x2l[:, ts], True, True,
                               x2l_ready)

            def base(u0, u1, k):
                n = K * (TU * u0 // T) + k
                cols, ts, x2l_ready = of_tokens(u0, u1)
                if n >= K:
                    pe.wait_ge(s["hl_ready"], 1 + max(m for m in range(n) if PS_HID[m] is PS_HID[n]))
                ks = slice(P * k, P * (k + 1))
                product(PS_HID[n][:, cols], wih[:, ks], wil[:, ks], x2h[:, ts], x2l[:, ts], cols.start == 0, False,
                        x2l_ready)

            def lora(c, k):
                pe.wait_ge(s["lowh_ready"], c + 1)
                ks = slice(P * k, P * (k + 1))
                product(PS_HID[K * c + k][:], b1h[:, ks], b1l[:, ks], lowh[:, chunk(c)], lowl[:, chunk(c)],
                        False, True, (s["lowl_ready"], c + 1)).then_inc(s["hid_done"], 1)

            def hidden_columns(n):
                step = STEPS[n]
                c = step["g0"] // GC
                return c, slice(P * (step["g0"] - GC * c), P * (step["g0"] - GC * c + step["n"])), P * step["n"]

            def to_mid(n, k):
                c, cols, w = hidden_columns(n)
                pe.wait_ge(s["hh_ready"], K * c + k + 1)
                ks = slice(P * k, P * (k + 1))
                m = product(STEPS[n]["mid"][:, 0:w], a2h[:, ks], a2l[:, ks], hh[:, c, k, cols], hl[:, c, k, cols],
                            k == 0, k == K - 1, (s["hl_ready"], K * c + k + 1))
                if k == K - 1:
                    m.then_inc(s["mid_done"], 1)

            def to_out(n, k):
                c, cols, w = hidden_columns(n)
                pe.wait_ge(s["hh_ready"], K * c + k + 1)
                ks = slice(P * k, P * (k + 1))
                product(STEPS[n]["out"][:, 0:w], woh[:, ks], wol[:, ks], hh[:, c, k, cols], hl[:, c, k, cols],
                        k == 0, False, (s["hl_ready"], K * c + k + 1))

            def up(n):
                pe.wait_ge(s["mid_ready"], n + 1)
                pe.matmul(STEPS[n]["out"][:, 0:P * STEPS[n]["n"]], wout[:, W_OUT["b"]], mid[:, step_tokens(STEPS[n])],
                          start=False, stop=True).then_inc(s["out_done"], 1)

            def mask(n):
                pe.matmul(STEPS[n]["score"][:, 0:S * STEPS[n]["n"]], ident,
                          pen[:, tiles(STEPS[n])].rearrange("p g l -> p (g l)"), start=True, stop=False)

            def attend(n):
                step = STEPS[n]
                w = S * step["n"]
                pe.wait_ge(s["x3_ready"], n + 1)
                x3v = x3[:, step_tokens(step)].rearrange("p (g q l) -> p q g l", q=Q, l=S)
                for q in range(Q):
                    last = pe.matmul(step["attn"][S * q:S * (q + 1), 0:w], pin[:, POOL["w1"]], x3v[:, q],
                                     start=True, stop=True)
                last.then_inc(s["attn_done"], 1)
                if n:
                    pe.wait_ge(s["x3n_ready"], n)
                for i in range(step["n"]):
                    g = step["g0"] + i
                    last = pe.transpose(step["turn"][:, P * i:P * (i + 1)], x3[:, P * g:P * (g + 1)], ident)
                last.then_inc(s["x3n_done"], 1)

            def score(n):
                step = STEPS[n]
                pe.wait_ge(s["attn_ready"], n + 1)
                pe.matmul(step["score"][:, 0:S * step["n"]], pin[:, POOL["v"]],
                          attn[:, tiles(step)].rearrange("p g l -> p (g l)"), start=False, stop=True)\
                    .then_inc(s["score_done"], 1)

            def pooled(n, i0, i1):
                step = STEPS[n]
                pe.wait_ge(s["et_ready"], n + 1)
                pe.wait_ge(s["x3n_ready"], n + 1)
                for i in range(i0, i1):
                    g = step["g0"] + i
                    pe.matmul(step["pool"][:, P * i:P * (i + 1)], et[:, g].rearrange("p q l -> p (q l)"), x3n[:, g],
                              start=True, stop=True).then_inc(s["pooled_done"], 1)

            pe.wait_ge(s["zeros_ready"], 1)
            keep_warm(WARM)
            pe.wait_ge(s["d_first"], 16)
            pe.wait_ge(s["d_x0"], 16)
            second_difference(0, 0).then_inc(s["second_done"], 1)
            second_difference(1, 0).then_inc(s["second_done"], 1)
            pe.wait_ge(s["d_common"], 16)
            pe.wait_ge(s["hot_ready"], 1)
            pe.matmul(PS_BIAS[:, 0:B], com[:, COMMON["bias"]], hot[:], start=True, stop=True)\
                .then_inc(s["bias_done"], 1)
            pe.matmul(PS_WI[:], com[:, COMMON["wi_a"]], com[:, COMMON["wi_b"]], start=True, stop=True)\
                .then_inc(s["wi_done"], 1)
            common_out(0)
            common_out(1)
            subject(0)
            common_out(2)
            common_out(3).then_inc(s["wo_done"], 1)
            keep_warm(1)
            pe.wait_ge(s["wb_helped"], 1)
            subject(1)
            turn_y(0)
            pe.wait_ge(s["d_x1"], 16)
            second_difference(2, 0)
            turn_y(1)
            second_difference(2, 1).then_inc(s["second_done"], 1)
            pe.wait_ge(s["a1h_ready"], 1)
            pe.wait_ge(s["a1l_ready"], 1)
            pe.wait_ge(s["bias_ready"], 1)
            down(0, 1)
            pe.wait_ge(s["wih_ready"], 1)
            pe.wait_ge(s["wil_ready"], 1)
            base(0, 1, 0)
            base(0, 1, 1)
            down(1, 2).then_inc(s["low_done"], 1)
            base(1, 2, 0)
            base(1, 2, 1)
            pe.wait_ge(s["across_ready"], len(PARTS))
            base(0, 2, 2)
            base(0, 2, 3)
            pe.wait_ge(s["b1h_ready"], 1)
            pe.wait_ge(s["b1l_ready"], 1)
            lora(0, 0)
            lora(0, 1)
            lora(0, 2)
            lora(0, 3)
            subject(2)
            pe.wait_ge(s["a2h_ready"], 1)
            pe.wait_ge(s["a2l_ready"], 1)
            to_mid(0, 0)
            to_mid(0, 1)
            turn_y(2)
            subject(3)
            pe.wait_ge(s["woh_ready"], 1)
            pe.wait_ge(s["wol_ready"], 1)
            to_out(0, 0)
            turn_y(3)
            to_out(0, 1)
            to_mid(0, 2)
            to_out(0, 2)
            to_mid(0, 3)
            down(2, 4).then_inc(s["low_done"], 1)
            to_out(0, 3)
            base(2, 4, 0)
            up(0)
            base(2, 4, 1)
            base(2, 4, 2)
            lora(1, 0)
            lora(1, 1)
            pe.wait_ge(s["d_pool"], 16)
            pe.wait_ge(s["pen_ready"], 1)
            pe.wait_ge(s["low_ready"], NC)
            mask(0)
            attend(0)
            lora(1, 2)
            score(0)
            base(2, 4, 3)
            lora(1, 3)
            for k in range(K - 1):
                to_mid(1, k)
            for k in range(K - 1):
                to_out(1, k)
            to_mid(1, K - 1)
            to_out(1, K - 1)
            for k in range(K):
                to_mid(2, k)
            up(1)
            mask(1)
            for k in range(2):
                to_out(2, k)
            attend(1)
            for k in range(2, K):
                to_out(2, k)
            score(1)
            up(2)
            pe.wait_ge(s["x3_ready"], 2)
            mask(2)
            pooled(0, 0, 2)
            attend(2)
            pooled(0, 2, 4)
            score(2)
            pooled(1, 0, 2)
            pooled(2, 0, 2)


def score_weights(v):
    import numpy as np

    w = np.zeros((P, P), v.dtype)
    for q in range(Q):
        w[A * q:A * (q + 1), S * q:S * (q + 1)] = v[:, None]
    return w


def kernel(x, condB_zX, condB_zY, condB_zR, itok_B_0_7, itok_B_0_2, L1_cond_weight, L1_cond_bias, L2_cond_wi,
           L2_cond_wo, L2_cond_common_wi_a, L2_cond_common_wi_b, L2_cond_common_wo_a, L2_cond_common_wo_b,
           L2_cond_experts_wi_a, L2_cond_experts_wi_b, L2_cond_experts_wo_a, L2_cond_experts_wo_b, L3_cond_W1,
           L3_cond_b1, L3_cond_v):
    import numpy as np
    import concourse.bacc as bacc
    from concourse.bass_utils import run_bass_kernel_spmd

    f32 = np.float32

    def side(*parts):
        return np.concatenate([np.asarray(p) for p in parts], axis=1)

    def everywhere(row):
        return np.tile(np.asarray(row), (P, 1))

    def per_row(a):
        return np.repeat(np.asarray(a).reshape(G, Q).T, S, axis=0)

    row = np.arange(P)
    second = np.zeros((D, D), f32)
    for d in range(D):
        second[d, d] = -2.0
        second[d - 1 if d else d + 1, d] += 1.0
        second[d + 1 if d < D - 1 else d - 1, d] += 1.0
    j, l = np.meshgrid(row % S, np.arange(S), indexing="ij")
    masks = [l != j, l <= j, l >= j]
    penalty = [np.where(m, 0.0, NEG).astype(f32) for m in masks]
    count = [m.sum(1, keepdims=True).astype(f32) for m in masks]
    against = lambda a: [a[0], a[1] - a[0], a[2] - a[0]]
    power = everywhere(D * E ** (np.arange(B) % WORD)).astype(np.int32)

    arrays = {
        "ids": side(everywhere(itok_B_0_7), per_row(itok_B_0_2), power),
        "first": side(everywhere(condB_zX), everywhere(condB_zY), everywhere(condB_zR), row[:, None].astype(f32),
                      (row // R)[:, None].astype(f32), second),
        "x_t": np.asarray(x).transpose(2, 0, 1).reshape(D, B * S),
        "w_subject": side(np.asarray(L1_cond_weight).transpose(2, 0, 1).reshape(D, E * D), np.eye(P, dtype=f32)),
        "common": side(*(np.pad(np.asarray(a), ((0, ROWS - a.shape[0]), (0, 0)))
                         for a in (L2_cond_common_wi_a, np.asarray(L2_cond_common_wi_b).T, L2_cond_common_wo_a,
                                   np.asarray(L2_cond_common_wo_b).T, L1_cond_bias))),
        "w_in": side(np.asarray(L2_cond_experts_wi_a).reshape(E * R, D).T, np.asarray(L2_cond_wi).T),
        "b_in": np.asarray(L2_cond_experts_wi_b).transpose(0, 2, 1).reshape(E * R, F),
        "w_out": side(np.asarray(L2_cond_wo).T.reshape(K, P, D).transpose(1, 0, 2).reshape(P, K * D),
                      np.asarray(L2_cond_experts_wo_a).transpose(2, 0, 1).reshape(K, P, E * R)
                      .transpose(1, 0, 2).reshape(P, K * E * R),
                      np.asarray(L2_cond_experts_wo_b).transpose(0, 2, 1).reshape(E * R, D)),
        "pool_in": side(L3_cond_W1, score_weights(np.asarray(L3_cond_v)), np.tile(np.asarray(L3_cond_b1), Q)[:, None],
                        *against(penalty), *against(count)),
    }
    nc = bacc.Bacc("TRN2", target_bir_lowering=False, num_devices=1)
    args = []
    for name, a in arrays.items():
        a = arrays[name] = np.ascontiguousarray(a)
        args.append(nc.dram_tensor(name, a.shape, mybir.dt.from_np(a.dtype), kind="ExternalInput").ap())
    out = nc.dram_tensor("out", (P, G, D), F32, kind="ExternalOutput").ap()
    program(nc, *args, out)
    got = run_bass_kernel_spmd(nc, [arrays], core_ids=[0]).results[0]["out"]
    return got.reshape(Q, S, G, D).transpose(2, 0, 1, 3).reshape(B, S, D)
```

```python
import concourse.bass as bass
from concourse import mybir
from contextlib import ExitStack

F32 = mybir.dt.float32
F32R = mybir.dt.float32r
I32 = mybir.dt.int32
ALU = mybir.AluOpType
ACT = mybir.ActivationFunctionType
AX = mybir.AxisListType

B, S, D = 32, 32, 128
E, R, F, A = 8, 16, 512, 32
P = 128
Q = P // S
G = B // Q
NC = 2
GC = G // NC
T = GC * P
NU = 4
GU = G // NU
BU = B // NU
TU = T * NC // NU
K = F // P
ROWS = 32
HELP = 3
WORD = 8
ALPHA = 2.0
NEG = -1e30


def columns(**widths):
    at, out = 0, {}
    for name, n in widths.items():
        out[name] = slice(at, at + n)
        at += n
    return out, at


PARTS = [(0, BU), (BU, BU), (2 * BU, 2 * BU)]
WARM = 8
IDS, N_IDS = columns(subject=B, mask=G, power=B)
FIRST, N_FIRST = columns(zX=B, zY=B, zR=B, row=1, expert=1, second=D)
SUBJECT, N_SUBJECT = columns(w=E * D, ident=P)
COMMON, N_COMMON = columns(wi_a=D, wi_b=F, wo_a=F, wo_b=D, bias=D)
W_IN, N_IN = columns(a=E * R, base=F)
W_OUT, N_OUT = columns(base=K * D, a=K * E * R, b=D)
POOL, N_POOL = columns(w1=A, v=P, b1=1, penalty=3 * S, count=3)


SEMAPHORES = [
    "d_x0", "d_x1", "d_ids", "d_first", "d_wsub", "d_common", "d_win", "d_bin", "d_wout", "d_pool", "d_out",
    "zeros_ready", "warm_ready", "prod_ready", "words_ready", "hot_ready",
    "centre_t_ready", "centre_ready", "near_ready", "along_ready", "grow_ready", "rest_ready", "second_done",
    "across_ready", "react_ready", "sums_ready", "x1_ready",
    "bias_done", "bias_ready", "wb_ready", "wb_helped", "x1b_ready", "y_done", "y_ready", "yt_done", "x2_ready",
    "x2h_ready", "x2l_ready",
    "expert_ready", "a1h_ready", "a1l_ready", "wi_done", "wi_ready", "wih_ready", "wil_ready", "b1h_ready",
    "b1l_ready", "wo_done", "wo_common_ready", "wo_ready", "woh_ready", "wol_ready", "a2h_ready", "a2l_ready",
    "b2h_ready", "b2l_ready",
    "low_done", "low_ready", "lowh_ready", "lowl_ready", "hid_done", "hh_ready", "hl_ready", "mid_done",
    "mid_ready", "midh_ready", "midl_ready", "out_done", "x3_ready",
    "type_ready", "pen_part_ready", "pen_sum_ready", "pen_ready", "cnt_part_ready", "cnt_sum_ready",
    "cnt_ready", "et_zeroed", "attn_done", "attn_ready", "x3n_done", "x3n_ready", "score_done", "smax_ready",
    "sd_ready", "e_ready", "et_ready", "esum_ready", "den_ready", "rden_ready", "pooled_done", "scaled_ready",
    "pool_res_ready", "res_ready",
]


def program(nc, ids, first, x_t, w_subject, common, w_in, b_in, w_out, pool_in, out):
    with ExitStack() as ctx:
        def sb(name, shape, dt=F32):
            return ctx.enter_context(nc.sbuf_tensor(name, shape, dt))

        def sem(name):
            return ctx.enter_context(nc.semaphore(name))

        ids_sb = sb("ids_sb", [P, N_IDS], I32)
        first_sb = sb("first_sb", [P, N_FIRST])
        x = sb("x", [P, B, S])
        wsub = sb("wsub", [P, N_SUBJECT])
        com = sb("com", [ROWS, N_COMMON])
        win = sb("win", [P, N_IN])
        bin_ = sb("bin_", [P, F])
        wout = sb("wout", [P, N_OUT])
        pin = sb("pin", [P, N_POOL])
        ident = wsub[:, SUBJECT["ident"]]
        zX, zY, zR = (first_sb[:, FIRST[n]] for n in ("zX", "zY", "zR"))

        warm = sb("warm", [P, 1])
        warmed = sb("warmed", [P, 1])
        zeros = sb("zeros", [P, P])
        centre_t = sb("centre_t", [P, B])
        centre = sb("centre", [P, B])
        near = sb("near", [P, B, S])
        along = sb("along", [P, B, S])
        grow = sb("grow", [P, B, S])
        rest = sb("rest", [P, B, S])
        react = sb("react", [P, B, S])
        across = sb("across", [P, B, S])
        sums = sb("sums", [P, B, S])
        x1 = sb("x1", [P, B, S])
        prod = sb("prod", [1, B])
        words = sb("words", [1, B // WORD], I32)
        hot = sb("hot", [ROWS, B])
        expert = sb("expert", [P, B])
        bias = sb("bias", [P, B])
        wb = sb("wb", [P, B, D])
        x1b = sb("x1b", [P, B, S])
        y = sb("y", [P, G, D])
        x2 = sb("x2", [P, NC * T])
        x2h = sb("x2h", [P, NC * T], F32R)
        x2l = sb("x2l", [P, NC * T], F32R)
        a1h, a1l = sb("a1h", [P, E * R], F32R), sb("a1l", [P, E * R], F32R)
        b1h, b1l = sb("b1h", [P, F], F32R), sb("b1l", [P, F], F32R)
        wi, wih, wil = sb("wi", [P, F]), sb("wih", [P, F], F32R), sb("wil", [P, F], F32R)
        wo_common = sb("wo_common", [P, K * D])
        wo, woh, wol = sb("wo", [P, K * D]), sb("woh", [P, K * D], F32R), sb("wol", [P, K * D], F32R)
        a2h, a2l = sb("a2h", [P, K * E * R], F32R), sb("a2l", [P, K * E * R], F32R)
        b2h, b2l = sb("b2h", [P, D], F32R), sb("b2l", [P, D], F32R)
        low, lowh, lowl = sb("low", [P, NC * T]), sb("lowh", [P, NC * T], F32R), sb("lowl", [P, NC * T], F32R)
        hh, hl = sb("hh", [P, NC, K, T], F32R), sb("hl", [P, NC, K, T], F32R)
        mid, midh, midl = sb("mid", [P, NC * T]), sb("midh", [P, NC * T], F32R), sb("midl", [P, NC * T], F32R)
        x3 = sb("x3", [P, NC * T])
        is_type = sb("is_type", [P, 2, G])
        pen_part = sb("pen_part", [P, 2, G, S])
        pen_sum = sb("pen_sum", [P, G, S])
        pen = sb("pen", [P, G, S])
        cnt_part = sb("cnt_part", [P, 2, G])
        cnt_sum = sb("cnt_sum", [P, G])
        cnt = sb("cnt", [P, G])
        attn = sb("attn", [P, G, S])
        smax = sb("smax", [P, G])
        sd = sb("sd", [P, G, S])
        e = sb("e", [P, G, S])
        esum = sb("esum", [P, G])
        den = sb("den", [P, G])
        rden = sb("rden", [P, G])
        et = sb("et", [P, G, Q, S])
        x3n = sb("x3n", [P, G, D])
        scaled = sb("scaled", [P, GC, D])
        res = sb("res", [P, G, D])

        bank = [ctx.enter_context(nc.psum_tensor(f"bank{i}", [P, T], F32)) for i in range(8)]
        PS_DIFF = [bank[0], bank[1], bank[5]]
        PS_YT = [bank[0], bank[1], bank[0], bank[1]]
        PS_Y = [bank[2], bank[3], bank[3], bank[3]]
        PS_HID = [bank[i] for i in (4, 2, 5, 1, 4, 2, 5, 4)]
        PS_LOW = [bank[6], bank[3]]
        PS_WARM, PS_WI, PS_WO, PS_BIAS = bank[5], bank[4], bank[7], bank[6]
        STEPS = [dict(g0=0, n=GC, out=bank[7], mid=bank[6], attn=bank[0], turn=bank[1], score=bank[3],
                      pool=[bank[2], bank[5]]),
                 dict(g0=GC, n=GC // 2, out=bank[7], mid=bank[6], attn=bank[0], turn=bank[1], score=bank[5],
                      pool=[bank[0]]),
                 dict(g0=GC + GC // 2, n=GC // 2, out=bank[4], mid=bank[2], attn=bank[3], turn=bank[6], score=bank[7],
                      pool=[bank[3]])]

        s = {n: sem(n) for n in SEMAPHORES}
        block = ctx.enter_context(nc.Block())

        def bcast(ap, axis, shape):
            return ap.unsqueeze(axis).to_broadcast(shape)

        def over_batch(ap):
            return bcast(ap, 2, [P, ap.shape[1], S])

        def by_batch(ap):
            return ap.rearrange("p (b s) -> p b s", s=S)

        def f32(ap):
            return ap.bitcast(F32)

        def batches(u):
            return slice(BU * u, BU * (u + 1))

        def part(i):
            return slice(PARTS[i][0], PARTS[i][0] + PARTS[i][1])

        def tokens(u):
            return slice(TU * u, TU * (u + 1))

        def tiles(step):
            return slice(step["g0"], step["g0"] + step["n"])

        def step_tokens(step):
            return slice(P * step["g0"], P * (step["g0"] + step["n"]))

        def load_words(engine, w0, w1):
            engine.wait_ge(s["words_ready"], 1)
            return nc.values_load_multi_w_load_instructions(
                words[0:1, w0:w1], engines=(engine.engine,), min_val=0, max_val=(E ** WORD - 1) * D)[1]

        def place(engine, word, b):
            return engine.snap((word >> (3 * (b % WORD))) & ((E - 1) * D))

        def pooled_rows(step, i):
            return step["pool"][i // 2][:, P * (i % 2):P * (i % 2 + 1)]

        @block.sync
        def _(sp):
            sp.dma_start(x[:, 0:B // 2], by_batch(x_t[:, 0:T])).then_inc(s["d_x0"], 16)
            sp.dma_start(wsub[:], w_subject).then_inc(s["d_wsub"], 16)
            sp.dma_start(com[:], common).then_inc(s["d_common"], 16)
            sp.dma_start(win[:], w_in).then_inc(s["d_win"], 16)
            sp.dma_start(bin_[:], b_in).then_inc(s["d_bin"], 16)
            sp.dma_start(x[:, B // 2:B], by_batch(x_t[:, T:2 * T])).then_inc(s["d_x1"], 16)
            sp.dma_start(wout[:], w_out).then_inc(s["d_wout"], 16)
            sp.dma_start(pin[:], pool_in).then_inc(s["d_pool"], 16)
            for n, (ready, count) in enumerate((("pool_res_ready", 2), ("res_ready", 2), ("res_ready", 4))):
                sp.wait_ge(s[ready], count)
                sp.dma_start(out[:, tiles(STEPS[n])], res[:, tiles(STEPS[n])]).then_inc(s["d_out"], 16)
            sp.wait_ge(s["d_out"], 16 * len(STEPS))

        @block.gpsimd
        def _(pool):
            def rate(i):
                bs = part(i)
                pool.tensor_tensor(grow[:, bs], x[:, bs], over_batch(zR[:, bs]), ALU.mult).then_inc(s["grow_ready"], 1)
                pool.wait_ge(s["grow_ready"], i + 1)
                pool.tensor_tensor(rest[:, bs], over_batch(centre[:, bs]), grow[:, bs], ALU.subtract)\
                    .then_inc(s["rest_ready"], 1)

            def add_bias(i):
                bs = part(i)
                pool.wait_ge(s["x1_ready"], i + 1)
                pool.tensor_tensor(x1b[:, bs], x1[:, bs], over_batch(bias[:, bs]), ALU.add).then_inc(s["x1b_ready"], 1)

            pool.dma_start(ids_sb[:], ids).then_inc(s["d_ids"], 16)
            pool.memset(et[:], 0.0).then_inc(s["et_zeroed"], 1)
            (word,) = load_words(pool, 1, 2)
            helped = [(b, place(pool, word, b)) for b in range(2 * BU - HELP, 2 * BU)]
            pool.wait_ge(s["d_first"], 16)
            pool.wait_ge(s["centre_ready"], 1)
            pool.wait_ge(s["d_x0"], 16)
            rate(0)
            rate(1)
            pool.wait_ge(s["d_wsub"], 16)
            for b, at in helped:
                last = pool.tensor_copy(wb[:, b], wsub[:, bass.ds(at, D)])
            last.then_inc(s["wb_helped"], 1)
            pool.wait_ge(s["bias_ready"], 1)
            add_bias(0)
            add_bias(1)
            pool.wait_ge(s["d_win"], 16)
            pool.wait_ge(s["a1h_ready"], 1)
            pool.tensor_tensor(a1l[:], win[:, W_IN["a"]], f32(a1h[:]), ALU.subtract).then_inc(s["a1l_ready"], 1)
            pool.wait_ge(s["wih_ready"], 1)
            for h in range(2):
                cols = slice(F // 2 * h, F // 2 * (h + 1))
                pool.tensor_tensor(wil[:, cols], wi[:, cols], f32(wih[:, cols]), ALU.subtract)\
                    .then_inc(s["wil_ready"], 1)
            pool.wait_ge(s["d_bin"], 16)
            pool.wait_ge(s["b1h_ready"], 1)
            pool.tensor_tensor(b1l[:], bin_[:], f32(b1h[:]), ALU.subtract).then_inc(s["b1l_ready"], 1)
            pool.wait_ge(s["d_x1"], 16)
            rate(2)
            pool.wait_ge(s["d_wout"], 16)
            pool.wait_ge(s["a2h_ready"], 1)
            pool.tensor_tensor(a2l[:], wout[:, W_OUT["a"]], f32(a2h[:]), ALU.subtract).then_inc(s["a2l_ready"], 1)
            pool.wait_ge(s["wo_common_ready"], 1)
            pool.tensor_tensor(wo[:], wo_common[:], wout[:, W_OUT["base"]], ALU.add).then_inc(s["wo_ready"], 1)
            add_bias(2)
            pool.wait_ge(s["woh_ready"], 1)
            pool.tensor_tensor(wol[:], wo[:], f32(woh[:]), ALU.subtract).then_inc(s["wol_ready"], 1)
            pool.wait_ge(s["type_ready"], 2)
            pool.wait_ge(s["d_pool"], 16)
            penalty = pin[:, POOL["penalty"]].rearrange("p (k l) -> p k l", k=3)
            for k in range(2):
                pool.tensor_tensor(pen_part[:, k], bcast(penalty[:, k + 1], 1, [P, G, S]),
                                   bcast(is_type[:, k], 2, [P, G, S]), ALU.mult).then_inc(s["pen_part_ready"], 1)
            pool.wait_ge(s["pen_part_ready"], 2)
            pool.tensor_tensor(pen_sum[:], pen_part[:, 0], pen_part[:, 1], ALU.add).then_inc(s["pen_sum_ready"], 1)
            pool.wait_ge(s["pen_sum_ready"], 1)
            pool.tensor_tensor(pen[:], pen_sum[:], bcast(penalty[:, 0], 1, [P, G, S]), ALU.add)\
                .then_inc(s["pen_ready"], 1)
            pool.wait_ge(s["b2h_ready"], 1)
            pool.tensor_tensor(b2l[:], wout[:, W_OUT["b"]], f32(b2h[:]), ALU.subtract).then_inc(s["b2l_ready"], 1)
            pool.wait_ge(s["x3n_ready"], 1)
            for h in range(2):
                gs = slice(2 * h, 2 * (h + 1))
                pool.wait_ge(s["scaled_ready"], gs.stop)
                pool.tensor_tensor(res[:, gs], scaled[:, gs], x3n[:, gs], ALU.add).then_inc(s["pool_res_ready"], 1)

        @block.scalar
        def _(act):
            def gather(b0, b1):
                for b in range(b0, b1):
                    at = place(act, loaded[b // WORD], b)
                    act.copy(wb[:, b], wsub[:, bass.ds(at, D)]).then_inc(s["wb_ready"], 1)

            def copy_y(u):
                act.wait_ge(s["y_done"], u + 1)
                act.copy(y[:, GU * u:GU * (u + 1)], PS_Y[u][:, 0:TU].rearrange("p (g d) -> p g d", g=GU))\
                    .then_inc(s["y_ready"], 1)

            def split_x2(u):
                act.wait_ge(s["x2_ready"], u + 1)
                act.copy(x2h[:, tokens(u)], x2[:, tokens(u)]).then_inc(s["x2h_ready"], 1)

            def split_low(c):
                act.wait_ge(s["low_ready"], c + 1)
                act.copy(lowh[:, T * c:T * (c + 1)], low[:, T * c:T * (c + 1)]).then_inc(s["lowh_ready"], 1)

            def relu(c, k):
                act.wait_ge(s["hid_done"], K * c + k + 1)
                act.activation(hh[:, c, k], PS_HID[K * c + k][:], ACT.Relu).then_inc(s["hh_ready"], 1)

            def split_mid(n):
                ts = step_tokens(STEPS[n])
                act.wait_ge(s["mid_ready"], n + 1)
                act.copy(midh[:, ts], mid[:, ts]).then_inc(s["midh_ready"], 1)

            def tanh(n):
                step = STEPS[n]
                act.wait_ge(s["attn_done"], n + 1)
                act.activation(attn[:, tiles(step)].rearrange("p g l -> p (g l)"), step["attn"][:, 0:S * step["n"]],
                               ACT.Tanh, bias=pin[:, POOL["b1"]]).then_inc(s["attn_ready"], 1)

            def copy_x3n(n):
                step = STEPS[n]
                act.wait_ge(s["x3n_done"], n + 1)
                act.copy(x3n[:, tiles(step)], step["turn"][:, 0:P * step["n"]].rearrange("p (g d) -> p g d", d=D))\
                    .then_inc(s["x3n_ready"], 1)

            def exp(n):
                act.wait_ge(s["sd_ready"], n + 1)
                act.activation(e[:, tiles(STEPS[n])], sd[:, tiles(STEPS[n])], ACT.Exp).then_inc(s["e_ready"], 1)

            def scale_pooled(i):
                act.wait_ge(s["rden_ready"], 1)
                act.wait_ge(s["pooled_done"], 2 * (i // 2 + 1))
                act.activation(scaled[:, i], pooled_rows(STEPS[0], i), ACT.Copy, scale=rden[:, i:i + 1])\
                    .then_inc(s["scaled_ready"], 1)

            act.dma_start(first_sb[:], first).then_inc(s["d_first"], 16)
            act.wait_ge(s["warm_ready"], 1)
            act.activation(warmed[:], warm[:], ACT.Tanh)
            loaded = load_words(act, 0, B // WORD)
            act.wait_ge(s["d_wsub"], 16)
            gather(0, 2 * BU - HELP)
            copy_y(0)
            act.wait_ge(s["d_win"], 16)
            act.copy(a1h[:], win[:, W_IN["a"]]).then_inc(s["a1h_ready"], 1)
            act.wait_ge(s["wi_ready"], 1)
            act.copy(wih[:], wi[:]).then_inc(s["wih_ready"], 1)
            copy_y(1)
            split_x2(0)
            act.wait_ge(s["d_bin"], 16)
            act.copy(b1h[:], bin_[:]).then_inc(s["b1h_ready"], 1)
            split_x2(1)
            gather(2 * BU, 2 * BU + 3)
            act.wait_ge(s["d_wout"], 16)
            act.copy(a2h[:], wout[:, W_OUT["a"]]).then_inc(s["a2h_ready"], 1)
            act.wait_ge(s["wo_done"], 1)
            act.activation(wo_common[:], PS_WO[:], ACT.Copy, scale=ALPHA).then_inc(s["wo_common_ready"], 1)
            split_low(0)
            gather(2 * BU + 3, 3 * BU)
            gather(3 * BU, 3 * BU + 2)
            relu(0, 0)
            relu(0, 1)
            gather(3 * BU + 2, 3 * BU + 4)
            relu(0, 2)
            act.wait_ge(s["wo_ready"], 1)
            act.copy(woh[:], wo[:]).then_inc(s["woh_ready"], 1)
            copy_y(2)
            gather(3 * BU + 4, 4 * BU)
            relu(0, 3)
            split_x2(2)
            copy_y(3)
            split_x2(3)
            act.copy(b2h[:], wout[:, W_OUT["b"]]).then_inc(s["b2h_ready"], 1)
            split_mid(0)
            split_low(1)
            relu(1, 0)
            relu(1, 1)
            act.wait_ge(s["d_pool"], 16)
            tanh(0)
            relu(1, 2)
            copy_x3n(0)
            relu(1, 3)
            exp(0)
            split_mid(1)
            split_mid(2)
            tanh(1)
            copy_x3n(1)
            exp(1)
            tanh(2)
            copy_x3n(2)
            scale_pooled(0)
            scale_pooled(1)
            scale_pooled(2)
            exp(2)
            scale_pooled(3)

        @block.vector
        def _(dve):
            def along_sequence(i):
                neighbours(i)
                scale_neighbours(i)

            def neighbours(i):
                bs = part(i)
                dve.tensor_tensor(near[:, bs, 1:S - 1], x[:, bs, 0:S - 2], x[:, bs, 2:S], ALU.add)\
                    .then_inc(s["near_ready"], 1)
                dve.tensor_scalar(near[:, bs, 0:S:S - 1], x[:, bs, 1:S - 1:S - 3], 2.0, None, ALU.mult)\
                    .then_inc(s["near_ready"], 1)

            def scale_neighbours(i):
                bs = part(i)
                dve.wait_ge(s["near_ready"], 2 * (i + 1))
                dve.tensor_tensor(along[:, bs], near[:, bs], over_batch(zY[:, bs]), ALU.mult)\
                    .then_inc(s["along_ready"], 1)

            def scale_second(i):
                bs = part(i)
                dve.wait_ge(s["second_done"], i + 1)
                dve.tensor_tensor(across[:, bs], by_batch(PS_DIFF[i][:, 0:S * PARTS[i][1]]), over_batch(zX[:, bs]),
                                  ALU.mult).then_inc(s["across_ready"], 1)

            def diffuse(i):
                bs = part(i)
                dve.wait_ge(s["rest_ready"], i + 1)
                dve.tensor_tensor(react[:, bs], rest[:, bs], x[:, bs], ALU.mult).then_inc(s["react_ready"], 1)
                dve.wait_ge(s["along_ready"], i + 1)
                dve.wait_ge(s["across_ready"], i + 1)
                dve.tensor_tensor(sums[:, bs], along[:, bs], across[:, bs], ALU.add).then_inc(s["sums_ready"], 1)
                dve.wait_ge(s["sums_ready"], i + 1)
                dve.wait_ge(s["react_ready"], i + 1)
                dve.tensor_tensor(x1[:, bs], sums[:, bs], react[:, bs], ALU.add).then_inc(s["x1_ready"], 1)

            def add_x2(u):
                dve.wait_ge(s["yt_done"], u + 1)
                dve.wait_ge(s["x1b_ready"], min(u, 2) + 1)
                dve.tensor_tensor(by_batch(x2[:, tokens(u)]), by_batch(PS_YT[u][:, 0:TU]), x1b[:, batches(u)], ALU.add)\
                    .then_inc(s["x2_ready"], 1)

            def split_x2(u):
                ts = tokens(u)
                dve.wait_ge(s["x2h_ready"], u + 1)
                dve.tensor_tensor(x2l[:, ts], x2[:, ts], f32(x2h[:, ts]), ALU.subtract).then_inc(s["x2l_ready"], 1)

            def pick_low(c):
                bs = slice(B // NC * c, B // NC * (c + 1))
                dve.wait_ge(s["low_done"], c + 1)
                dve.tensor_tensor(by_batch(low[:, T * c:T * (c + 1)]), by_batch(PS_LOW[c][:]),
                                  over_batch(expert[:, bs]), ALU.mult).then_inc(s["low_ready"], 1)

            def split_low(c):
                ts = slice(T * c, T * (c + 1))
                dve.wait_ge(s["lowh_ready"], c + 1)
                dve.tensor_tensor(lowl[:, ts], low[:, ts], f32(lowh[:, ts]), ALU.subtract).then_inc(s["lowl_ready"], 1)

            def relu_rest(c, k):
                dve.wait_ge(s["hh_ready"], K * c + k + 1)
                dve.scalar_tensor_tensor(out=hl[:, c, k], in0=PS_HID[K * c + k][:], scalar=0.0,
                                         in1=f32(hh[:, c, k]), op0=ALU.max, op1=ALU.subtract).then_inc(s["hl_ready"], 1)

            def pick_mid(n):
                step = STEPS[n]
                bs = slice(Q * step["g0"], Q * (step["g0"] + step["n"]))
                dve.wait_ge(s["mid_done"], n + 1)
                dve.tensor_tensor(by_batch(mid[:, step_tokens(step)]), by_batch(step["mid"][:, 0:P * step["n"]]),
                                  over_batch(expert[:, bs]), ALU.mult).then_inc(s["mid_ready"], 1)

            def split_mid(n):
                ts = step_tokens(STEPS[n])
                dve.wait_ge(s["midh_ready"], n + 1)
                dve.tensor_tensor(midl[:, ts], mid[:, ts], f32(midh[:, ts]), ALU.subtract).then_inc(s["midl_ready"], 1)

            def add_x3(n):
                step = STEPS[n]
                ts = step_tokens(step)
                dve.wait_ge(s["out_done"], n + 1)
                dve.tensor_tensor(x3[:, ts], step["out"][:, 0:P * step["n"]], x2[:, ts], ALU.add)\
                    .then_inc(s["x3_ready"], 1)

            def softmax(n):
                step = STEPS[n]
                gs, w = tiles(step), step["n"]
                masked = step["score"][:, 0:S * w].rearrange("p (g l) -> p g l", g=w)
                dve.wait_ge(s["score_done"], n + 1)
                dve.tensor_reduce(smax[:, gs], masked, AX.X, ALU.max).then_inc(s["smax_ready"], 1)
                dve.wait_ge(s["smax_ready"], n + 1)
                dve.tensor_tensor(sd[:, gs], masked, bcast(smax[:, gs], 2, [P, w, S]), ALU.subtract)\
                    .then_inc(s["sd_ready"], 1)

            def turn(n):
                gs = tiles(STEPS[n])
                dve.wait_ge(s["e_ready"], n + 1)
                for q in range(Q):
                    qs = slice(S * q, S * (q + 1))
                    last = dve.transpose(et[qs, gs, q, :], e[qs, gs])
                last.then_inc(s["et_ready"], 1)

            def sum_up(n):
                gs = tiles(STEPS[n])
                dve.tensor_reduce(esum[:, gs], e[:, gs], AX.X, ALU.add).then_inc(s["esum_ready"], 1)

            def denominators(n):
                gs = tiles(STEPS[n])
                dve.wait_ge(s["esum_ready"], n + 1)
                dve.tensor_tensor(den[:, gs], esum[:, gs], cnt[:, gs], ALU.mult).then_inc(s["den_ready"], 1)
                dve.wait_ge(s["den_ready"], n + 1)
                dve.reciprocal(rden[:, gs], den[:, gs]).then_inc(s["rden_ready"], 1)

            def finish(n, i0, i1):
                step = STEPS[n]
                dve.wait_ge(s["rden_ready"], n + 1)
                dve.wait_ge(s["pooled_done"], step["g0"] + step["n"])
                dve.wait_ge(s["x3n_ready"], n + 1)
                for i in range(i0, i1):
                    g = step["g0"] + i
                    dve.scalar_tensor_tensor(out=res[:, g], in0=pooled_rows(step, i),
                                             scalar=rden[:, g:g + 1], in1=x3n[:, g], op0=ALU.mult,
                                             op1=ALU.add).then_inc(s["res_ready"], 1)

            dve.memset(zeros[:], 0.0).then_inc(s["zeros_ready"], 1)
            dve.memset(warm[:], 0.0).then_inc(s["warm_ready"], 1)
            dve.wait_ge(s["d_ids"], 16)
            dve.tensor_tensor(prod[:], ids_sb[0:1, IDS["subject"]], ids_sb[0:1, IDS["power"]], ALU.mult)\
                .then_inc(s["prod_ready"], 1)
            dve.wait_ge(s["prod_ready"], 1)
            with nc.allow_low_precision(reason="multiples of D below 2 ** 24 of it are exact in float32"):
                dve.tensor_reduce(words[:], prod[:].rearrange("p (w k) -> p w k", k=WORD), AX.X, ALU.add)\
                    .then_inc(s["words_ready"], 1)
            dve.wait_ge(s["d_first"], 16)
            dve.tensor_scalar(hot[:], ids_sb[0:ROWS, IDS["subject"]], first_sb[0:ROWS, FIRST["row"]], None,
                              ALU.is_equal)\
                .then_inc(s["hot_ready"], 1)
            dve.scalar_tensor_tensor(out=centre_t[:], in0=zY, scalar=-2.0, in1=zR, op0=ALU.mult, op1=ALU.add)\
                .then_inc(s["centre_t_ready"], 1)
            dve.wait_ge(s["centre_t_ready"], 1)
            dve.tensor_scalar(centre[:], centre_t[:], 1.0, None, ALU.add).then_inc(s["centre_ready"], 1)
            dve.wait_ge(s["d_x0"], 16)
            along_sequence(0)
            neighbours(1)
            scale_second(0)
            diffuse(0)
            dve.wait_ge(s["bias_done"], 1)
            dve.tensor_copy(bias[:], PS_BIAS[:, 0:B]).then_inc(s["bias_ready"], 1)
            scale_neighbours(1)
            scale_second(1)
            diffuse(1)
            dve.wait_ge(s["wi_done"], 1)
            dve.wait_ge(s["d_win"], 16)
            dve.scalar_tensor_tensor(out=wi[:], in0=PS_WI[:], scalar=ALPHA, in1=win[:, W_IN["base"]],
                                     op0=ALU.mult, op1=ALU.add).then_inc(s["wi_ready"], 1)
            dve.wait_ge(s["d_x1"], 16)
            neighbours(2)
            dve.tensor_scalar(expert[:], ids_sb[:, IDS["subject"]], first_sb[:, FIRST["expert"]], ALPHA, ALU.is_equal,
                              ALU.mult).then_inc(s["expert_ready"], 1)
            add_x2(0)
            add_x2(1)
            split_x2(0)
            split_x2(1)
            scale_second(2)
            dve.wait_ge(s["expert_ready"], 1)
            pick_low(0)
            scale_neighbours(2)
            split_low(0)
            diffuse(2)
            relu_rest(0, 0)
            for k in range(2):
                dve.tensor_scalar(is_type[:, k], ids_sb[:, IDS["mask"]], float(k), None, ALU.is_equal)\
                    .then_inc(s["type_ready"], 1)
            relu_rest(0, 1)
            relu_rest(0, 2)
            add_x2(2)
            relu_rest(0, 3)
            split_x2(2)
            add_x2(3)
            split_x2(3)
            count = pin[:, POOL["count"]]
            dve.wait_ge(s["d_pool"], 16)
            dve.wait_ge(s["type_ready"], 2)
            for k in range(2):
                dve.tensor_scalar(cnt_part[:, k], is_type[:, k], count[:, k + 1:k + 2], None, ALU.mult)\
                    .then_inc(s["cnt_part_ready"], 1)
            dve.wait_ge(s["cnt_part_ready"], 2)
            dve.tensor_tensor(cnt_sum[:], cnt_part[:, 0], cnt_part[:, 1], ALU.add).then_inc(s["cnt_sum_ready"], 1)
            dve.wait_ge(s["cnt_sum_ready"], 1)
            dve.tensor_scalar(cnt[:], cnt_sum[:], count[:, 0:1], None, ALU.add).then_inc(s["cnt_ready"], 1)
            pick_mid(0)
            pick_low(1)
            split_mid(0)
            split_low(1)
            add_x3(0)
            relu_rest(1, 0)
            relu_rest(1, 1)
            relu_rest(1, 2)
            softmax(0)
            relu_rest(1, 3)
            dve.wait_ge(s["et_zeroed"], 1)
            dve.wait_ge(s["cnt_ready"], 1)
            turn(0)
            sum_up(0)
            denominators(0)
            pick_mid(1)
            split_mid(1)
            pick_mid(2)
            add_x3(1)
            split_mid(2)
            add_x3(2)
            softmax(1)
            turn(1)
            sum_up(1)
            softmax(2)
            denominators(1)
            turn(2)
            sum_up(2)
            finish(1, 0, 1)
            denominators(2)
            finish(1, 1, 2)
            finish(2, 0, 2)

        @block.tensor
        def _(pe):
            def high(o, wh, wl, vh, vl, start, stop):
                pe.matmul(o, wh, vh, start=start, stop=False)
                pe.matmul(o, wl, vh, start=False, stop=False)

            def products(*which, vl_ready):
                for p in which:
                    high(*p)
                pe.wait_ge(*vl_ready)
                return [pe.matmul(o, wh, vl, start=False, stop=stop) for o, wh, wl, vh, vl, start, stop in which]

            def keep_warm(n):
                for _ in range(n):
                    pe.matmul(PS_WARM[:, 0:P], zeros[:, 0:P], zeros[:, 0:P], start=True, stop=True)

            def second_difference(i, h):
                b0 = PARTS[i][0] + BU * h
                return pe.matmul(PS_DIFF[i][:, TU * h:TU * (h + 1)], first_sb[:, FIRST["second"]], x[:, b0:b0 + BU],
                                 start=True, stop=True)

            def common_out(k):
                wo_a = com[:, COMMON["wo_a"]]
                return pe.matmul(PS_WO[:, D * k:D * (k + 1)], wo_a[:, P * k:P * (k + 1)], com[:, COMMON["wo_b"]],
                                 start=True, stop=True)

            def subject(u):
                pe.wait_ge(s["wb_ready"], BU * (u + 1) - (HELP if u else 0))
                pe.wait_ge(s["x1_ready"], min(u, 2) + 1)
                if u >= 2:
                    pe.wait_ge(s["y_ready"], u)
                for g in range(GU):
                    for q in range(Q):
                        b = BU * u + Q * g + q
                        last = pe.matmul(PS_Y[u][S * q:S * (q + 1), D * g:D * (g + 1)], x1[:, b], wb[:, b],
                                         start=True, stop=True)
                last.then_inc(s["y_done"], 1)

            def turn_y(u):
                pe.wait_ge(s["y_ready"], u + 1)
                if PS_YT[u] is PS_HID[K - 1] and u >= 2:
                    pe.wait_ge(s["hl_ready"], K)
                for g in range(GU):
                    last = pe.transpose(PS_YT[u][:, P * g:P * (g + 1)], y[:, GU * u + g], ident)
                last.then_inc(s["yt_done"], 1)

            def chunk(c):
                return slice(T * c, T * (c + 1))

            def of_tokens(u0, u1):
                t0 = T * (TU * u0 // T)
                return slice(TU * u0 - t0, TU * u1 - t0), slice(TU * u0, TU * u1)

            def down(u0, u1):
                cols, ts = of_tokens(u0, u1)
                return PS_LOW[TU * u0 // T][:, cols], a1h[:], a1l[:], x2h[:, ts], x2l[:, ts], True, True

            def base(u0, u1, k):
                cols, ts = of_tokens(u0, u1)
                ks = slice(P * k, P * (k + 1))
                return (PS_HID[K * (TU * u0 // T) + k][:, cols], wih[:, ks], wil[:, ks], x2h[:, ts], x2l[:, ts],
                        cols.start == 0, False)

            def x2_products(u0, u1, *which):
                pe.wait_ge(s["x2h_ready"], u1)
                return products(*which, vl_ready=(s["x2l_ready"], u1))

            def bank_of(c, k):
                n = K * c + k
                pe.wait_ge(s["hl_ready"], 1 + max(m for m in range(n) if PS_HID[m] is PS_HID[n]))

            def lora(c, *blocks):
                ts = chunk(c)
                pe.wait_ge(s["lowh_ready"], c + 1)
                for last in products(*[(PS_HID[K * c + k][:], b1h[:, P * k:P * (k + 1)], b1l[:, P * k:P * (k + 1)],
                                        lowh[:, ts], lowl[:, ts], False, True) for k in blocks],
                                     vl_ready=(s["lowl_ready"], c + 1)):
                    last.then_inc(s["hid_done"], 1)

            def hidden_columns(n):
                step = STEPS[n]
                c = step["g0"] // GC
                return c, slice(P * (step["g0"] - GC * c), P * (step["g0"] - GC * c + step["n"])), P * step["n"]

            def to_mid(n, k):
                c, cols, w = hidden_columns(n)
                pe.wait_ge(s["hh_ready"], K * c + k + 1)
                ks = slice(P * k, P * (k + 1))
                (last,) = products((STEPS[n]["mid"][:, 0:w], a2h[:, ks], a2l[:, ks], hh[:, c, k, cols],
                                    hl[:, c, k, cols], k == 0, k == K - 1), vl_ready=(s["hl_ready"], K * c + k + 1))
                if k == K - 1:
                    last.then_inc(s["mid_done"], 1)

            def to_out(n, k):
                c, cols, w = hidden_columns(n)
                pe.wait_ge(s["hh_ready"], K * c + k + 1)
                ks = slice(P * k, P * (k + 1))
                products((STEPS[n]["out"][:, 0:w], woh[:, ks], wol[:, ks], hh[:, c, k, cols], hl[:, c, k, cols],
                          k == 0, False), vl_ready=(s["hl_ready"], K * c + k + 1))

            def up(n):
                ts = step_tokens(STEPS[n])
                pe.wait_ge(s["midh_ready"], n + 1)
                (last,) = products((STEPS[n]["out"][:, 0:P * STEPS[n]["n"]], b2h[:], b2l[:], midh[:, ts], midl[:, ts],
                                    False, True), vl_ready=(s["midl_ready"], n + 1))
                last.then_inc(s["out_done"], 1)

            def mask(n):
                pe.matmul(STEPS[n]["score"][:, 0:S * STEPS[n]["n"]], ident,
                          pen[:, tiles(STEPS[n])].rearrange("p g l -> p (g l)"), start=True, stop=False)

            def attend(n):
                step = STEPS[n]
                w = S * step["n"]
                pe.wait_ge(s["x3_ready"], n + 1)
                x3v = x3[:, step_tokens(step)].rearrange("p (g q l) -> p q g l", q=Q, l=S)
                for q in range(Q):
                    last = pe.matmul(step["attn"][S * q:S * (q + 1), 0:w], pin[:, POOL["w1"]], x3v[:, q],
                                     start=True, stop=True)
                last.then_inc(s["attn_done"], 1)
                if n:
                    pe.wait_ge(s["x3n_ready"], n)
                for i in range(step["n"]):
                    g = step["g0"] + i
                    last = pe.transpose(step["turn"][:, P * i:P * (i + 1)], x3[:, P * g:P * (g + 1)], ident)
                last.then_inc(s["x3n_done"], 1)

            def score(n):
                step = STEPS[n]
                pe.wait_ge(s["attn_ready"], n + 1)
                pe.matmul(step["score"][:, 0:S * step["n"]], pin[:, POOL["v"]],
                          attn[:, tiles(step)].rearrange("p g l -> p (g l)"), start=False, stop=True)\
                    .then_inc(s["score_done"], 1)

            def pooled(n, i0, i1):
                step = STEPS[n]
                pe.wait_ge(s["et_ready"], n + 1)
                pe.wait_ge(s["x3n_ready"], n + 1)
                for i in range(i0, i1):
                    g = step["g0"] + i
                    pe.matmul(pooled_rows(step, i), et[:, g].rearrange("p q l -> p (q l)"), x3n[:, g],
                              start=True, stop=True).then_inc(s["pooled_done"], 1)

            pe.wait_ge(s["zeros_ready"], 1)
            keep_warm(WARM)
            pe.wait_ge(s["d_first"], 16)
            pe.wait_ge(s["d_x0"], 16)
            second_difference(0, 0).then_inc(s["second_done"], 1)
            second_difference(1, 0).then_inc(s["second_done"], 1)
            pe.wait_ge(s["d_common"], 16)
            pe.wait_ge(s["hot_ready"], 1)
            pe.matmul(PS_BIAS[:, 0:B], com[:, COMMON["bias"]], hot[:], start=True, stop=True)\
                .then_inc(s["bias_done"], 1)
            common_out(0)
            pe.matmul(PS_WI[:], com[:, COMMON["wi_a"]], com[:, COMMON["wi_b"]], start=True, stop=True)\
                .then_inc(s["wi_done"], 1)
            subject(0)
            for k in range(1, K):
                last = common_out(k)
            last.then_inc(s["wo_done"], 1)
            pe.wait_ge(s["wb_helped"], 1)
            subject(1)
            turn_y(0)
            pe.wait_ge(s["d_x1"], 16)
            second_difference(2, 0)
            turn_y(1)
            second_difference(2, 1).then_inc(s["second_done"], 1)
            pe.wait_ge(s["a1h_ready"], 1)
            pe.wait_ge(s["a1l_ready"], 1)
            pe.wait_ge(s["bias_ready"], 1)
            pe.wait_ge(s["wih_ready"], 1)
            pe.wait_ge(s["wil_ready"], 1)
            x2_products(0, 1, down(0, 1), base(0, 1, 0), base(0, 1, 1))
            x2_products(1, 2, down(1, 2))[0].then_inc(s["low_done"], 1)
            x2_products(1, 2, base(1, 2, 0))
            x2_products(1, 2, base(1, 2, 1))
            pe.wait_ge(s["across_ready"], len(PARTS))
            pe.wait_ge(s["wil_ready"], 2)
            x2_products(0, 2, base(0, 2, 2))
            x2_products(0, 2, base(0, 2, 3))
            pe.wait_ge(s["b1h_ready"], 1)
            pe.wait_ge(s["b1l_ready"], 1)
            lora(0, 0, 1)
            lora(0, 2)
            lora(0, 3)
            subject(2)
            pe.wait_ge(s["a2h_ready"], 1)
            pe.wait_ge(s["a2l_ready"], 1)
            to_mid(0, 0)
            to_mid(0, 1)
            turn_y(2)
            subject(3)
            pe.wait_ge(s["woh_ready"], 1)
            pe.wait_ge(s["wol_ready"], 1)
            to_out(0, 0)
            turn_y(3)
            to_out(0, 1)
            to_mid(0, 2)
            to_out(0, 2)
            to_mid(0, 3)
            pe.wait_ge(s["y_ready"], NU)
            x2_products(2, 4, down(2, 4))[0].then_inc(s["low_done"], 1)
            to_out(0, 3)
            bank_of(1, 0)
            x2_products(2, 4, base(2, 4, 0))
            bank_of(1, 1)
            x2_products(2, 4, base(2, 4, 1))
            pe.wait_ge(s["b2h_ready"], 1)
            pe.wait_ge(s["b2l_ready"], 1)
            up(0)
            bank_of(1, 2)
            x2_products(2, 4, base(2, 4, 2))
            lora(1, 0)
            lora(1, 1)
            pe.wait_ge(s["d_pool"], 16)
            pe.wait_ge(s["pen_ready"], 1)
            pe.wait_ge(s["low_ready"], NC)
            mask(0)
            attend(0)
            lora(1, 2)
            score(0)
            bank_of(1, 3)
            x2_products(2, 4, base(2, 4, 3))
            lora(1, 3)
            for k in range(K - 1):
                to_mid(1, k)
            for k in range(K - 1):
                to_out(1, k)
            to_mid(1, K - 1)
            to_out(1, K - 1)
            for k in range(K):
                to_mid(2, k)
            to_out(2, 0)
            up(1)
            mask(1)
            to_out(2, 1)
            to_out(2, 2)
            attend(1)
            to_out(2, 3)
            up(2)
            score(1)
            pe.wait_ge(s["x3_ready"], 2)
            mask(2)
            pooled(0, 0, 1)
            attend(2)
            pooled(0, 1, 2)
            pe.wait_ge(s["sd_ready"], 2)
            pooled(0, 2, 3)
            score(2)
            pooled(0, 3, 4)
            pooled(1, 0, 2)
            pooled(2, 0, 2)


def score_weights(v):
    import numpy as np

    w = np.zeros((P, P), v.dtype)
    for q in range(Q):
        w[A * q:A * (q + 1), S * q:S * (q + 1)] = v[:, None]
    return w


def kernel(x, condB_zX, condB_zY, condB_zR, itok_B_0_7, itok_B_0_2, L1_cond_weight, L1_cond_bias, L2_cond_wi,
           L2_cond_wo, L2_cond_common_wi_a, L2_cond_common_wi_b, L2_cond_common_wo_a, L2_cond_common_wo_b,
           L2_cond_experts_wi_a, L2_cond_experts_wi_b, L2_cond_experts_wo_a, L2_cond_experts_wo_b, L3_cond_W1,
           L3_cond_b1, L3_cond_v):
    import numpy as np
    import concourse.bacc as bacc
    from concourse.bass_utils import run_bass_kernel_spmd

    f32 = np.float32

    def side(*parts):
        return np.concatenate([np.asarray(p) for p in parts], axis=1)

    def everywhere(row):
        return np.tile(np.asarray(row), (P, 1))

    def per_row(a):
        return np.repeat(np.asarray(a).reshape(G, Q).T, S, axis=0)

    row = np.arange(P)
    second = np.zeros((D, D), f32)
    for d in range(D):
        second[d, d] = -2.0
        second[d - 1 if d else d + 1, d] += 1.0
        second[d + 1 if d < D - 1 else d - 1, d] += 1.0
    j, l = np.meshgrid(row % S, np.arange(S), indexing="ij")
    masks = [l != j, l <= j, l >= j]
    penalty = [np.where(m, 0.0, NEG).astype(f32) for m in masks]
    count = [m.sum(1, keepdims=True).astype(f32) for m in masks]
    against = lambda a: [a[0], a[1] - a[0], a[2] - a[0]]
    power = everywhere(D * E ** (np.arange(B) % WORD)).astype(np.int32)

    arrays = {
        "ids": side(everywhere(itok_B_0_7), per_row(itok_B_0_2), power),
        "first": side(everywhere(condB_zX), everywhere(condB_zY), everywhere(condB_zR), row[:, None].astype(f32),
                      (row // R)[:, None].astype(f32), second),
        "x_t": np.asarray(x).transpose(2, 0, 1).reshape(D, B * S),
        "w_subject": side(np.asarray(L1_cond_weight).transpose(2, 0, 1).reshape(D, E * D), np.eye(P, dtype=f32)),
        "common": side(*(np.pad(np.asarray(a), ((0, ROWS - a.shape[0]), (0, 0)))
                         for a in (L2_cond_common_wi_a, np.asarray(L2_cond_common_wi_b).T, L2_cond_common_wo_a,
                                   np.asarray(L2_cond_common_wo_b).T, L1_cond_bias))),
        "w_in": side(np.asarray(L2_cond_experts_wi_a).reshape(E * R, D).T, np.asarray(L2_cond_wi).T),
        "b_in": np.asarray(L2_cond_experts_wi_b).transpose(0, 2, 1).reshape(E * R, F),
        "w_out": side(np.asarray(L2_cond_wo).T.reshape(K, P, D).transpose(1, 0, 2).reshape(P, K * D),
                      np.asarray(L2_cond_experts_wo_a).transpose(2, 0, 1).reshape(K, P, E * R)
                      .transpose(1, 0, 2).reshape(P, K * E * R),
                      np.asarray(L2_cond_experts_wo_b).transpose(0, 2, 1).reshape(E * R, D)),
        "pool_in": side(L3_cond_W1, score_weights(np.asarray(L3_cond_v)), np.tile(np.asarray(L3_cond_b1), Q)[:, None],
                        *against(penalty), *against(count)),
    }
    nc = bacc.Bacc("TRN2", target_bir_lowering=False, num_devices=1)
    args = []
    for name, a in arrays.items():
        a = arrays[name] = np.ascontiguousarray(a)
        args.append(nc.dram_tensor(name, a.shape, mybir.dt.from_np(a.dtype), kind="ExternalInput").ap())
    out = nc.dram_tensor("out", (P, G, D), F32, kind="ExternalOutput").ap()
    program(nc, *args, out)
    got = run_bass_kernel_spmd(nc, [arrays], core_ids=[0]).results[0]["out"]
    return got.reshape(Q, S, G, D).transpose(2, 0, 1, 3).reshape(B, S, D)
```
